# Optimizing a Trainium2 kernel written in Bass

```python
import numpy as np
import jax
import jax.numpy as jnp

def _softmax(x, axis=-1):
    return jax.nn.softmax(x, axis=axis)

def _gelu(x):
    return jax.nn.gelu(x, approximate=True)

def _silu(x):
    return jax.nn.silu(x)

def _sigmoid(x):
    return jax.nn.sigmoid(x)

def _layernorm(x, axis=-1, eps=1e-05):
    m = jnp.mean(x, axis=axis, keepdims=True)
    v = jnp.var(x, axis=axis, keepdims=True)
    return (x - m) / jnp.sqrt(v + eps)

def _scatter_add(tgt, idx, src, axis=0):
    return tgt.at[idx].add(src)

def _segment_sum(src, seg, n):
    return jax.ops.segment_sum(src, seg, n)
kernel_name = 'mk_sandwich_d1_jaxref_r8_233588'

def setup_inputs(seed: int=0):
    np.random.seed(seed)
    _w = jnp.asarray

    def _L0_attn_setup():
        import jax, jax.numpy as jnp
        import numpy as np
        B, S, H = (2, 256, 128)
        NQ, NKV, HD, RANK = (16, 4, 64, 8)
        THETA = 10000.0
        LORA_SCALE = 16 / RANK
        ATTN_SCALE = 1.0 / np.sqrt(HD)

        def _lora_proj(x, W, A, Bm):
            return x @ W.T + x @ A.T @ Bm.T * LORA_SCALE

        def _rope(x, cos_h, sin_h):
            x1, x2 = (x[..., ::2], x[..., 1::2])
            return jnp.concatenate([x1 * cos_h - x2 * sin_h, x1 * sin_h + x2 * cos_h], axis=-1)

        def _forward(x, Wq, Wk, Wv, Wo, qA, qB, kA, kB, vA, vB, oA, oB):
            b, s, _ = x.shape
            q = _lora_proj(x, Wq, qA, qB).reshape(b, s, NQ, HD).transpose(0, 2, 1, 3)
            k = _lora_proj(x, Wk, kA, kB).reshape(b, s, NKV, HD).transpose(0, 2, 1, 3)
            v = _lora_proj(x, Wv, vA, vB).reshape(b, s, NKV, HD).transpose(0, 2, 1, 3)
            inv_freq = 1.0 / THETA ** (jnp.arange(0, HD, 2, dtype=jnp.float32) / HD)
            freqs = jnp.arange(s, dtype=jnp.float32)[:, None] * inv_freq[None, :]
            cos_h = jnp.cos(freqs)[None, None]
            sin_h = jnp.sin(freqs)[None, None]
            q = _rope(q, cos_h, sin_h)
            k = _rope(k, cos_h, sin_h)
            rep = NQ // NKV
            k = jnp.repeat(k, rep, axis=1)
            v = jnp.repeat(v, rep, axis=1)
            attn = jax.nn.softmax(jnp.einsum('bhqd,bhkd->bhqk', q, k) * ATTN_SCALE, axis=-1)
            out = jnp.einsum('bhqk,bhkd->bhqd', attn, v)
            out = out.transpose(0, 2, 1, 3).reshape(b, s, NQ * HD)
            return _lora_proj(out, Wo, oA, oB)
        key = jax.random.key(seed)
        ks = jax.random.split(key, 14)
        n = lambda k, shape, s: jax.random.normal(k, shape, jnp.float32) * s
        return {'x': n(ks[0], (B, S, H), 1.0), 'Wq': n(ks[1], (NQ * HD, H), 0.02), 'Wk': n(ks[2], (NKV * HD, H), 0.02), 'Wv': n(ks[3], (NKV * HD, H), 0.02), 'Wo': n(ks[4], (H, NQ * HD), 0.02), 'qA': n(ks[5], (RANK, H), 0.05), 'qB': n(ks[6], (NQ * HD, RANK), 0.05), 'kA': n(ks[7], (RANK, H), 0.05), 'kB': n(ks[8], (NKV * HD, RANK), 0.05), 'vA': n(ks[9], (RANK, H), 0.05), 'vB': n(ks[10], (NKV * HD, RANK), 0.05), 'oA': n(ks[11], (RANK, NQ * HD), 0.05), 'oB': n(ks[12], (H, RANK), 0.05)}
    _L0_attn_in = _L0_attn_setup()

    def _L0_ffn_setup():
        import jax, jax.numpy as jnp
        import numpy as np
        B, S, D = (4, 64, 128)
        E, K, H = (64, 8, 32)
        ES, HS = (2, 256)
        key = jax.random.key(seed)
        ks = jax.random.split(key, 8)
        scale = 0.02
        rn = lambda k, shape, s: jax.random.normal(k, shape, jnp.float32) * s
        return {'x': rn(ks[0], (B, S, D), 1.0), 'router_w': rn(ks[1], (D, E), scale), 'router_b': jnp.zeros((E,), jnp.float32), 'w1': rn(ks[2], (E, D, H), scale), 'b1': jnp.zeros((E, H), jnp.float32), 'w2': rn(ks[3], (E, H, D), scale), 'b2': jnp.zeros((E, D), jnp.float32), 'sw1': rn(ks[4], (ES, D, HS), scale), 'sb1': jnp.zeros((ES, HS), jnp.float32), 'sw2': rn(ks[5], (ES, HS, D), scale), 'sb2': jnp.zeros((ES, D), jnp.float32)}
    _L0_ffn_in = _L0_ffn_setup()
    _d = {'L0_attn_x': _L0_attn_in['x'], 'L0_attn_Wq': _L0_attn_in['Wq'], 'L0_attn_Wk': _L0_attn_in['Wk'], 'L0_attn_Wv': _L0_attn_in['Wv'], 'L0_attn_Wo': _L0_attn_in['Wo'], 'L0_attn_qA': _L0_attn_in['qA'], 'L0_attn_qB': _L0_attn_in['qB'], 'L0_attn_kA': _L0_attn_in['kA'], 'L0_attn_kB': _L0_attn_in['kB'], 'L0_attn_vA': _L0_attn_in['vA'], 'L0_attn_vB': _L0_attn_in['vB'], 'L0_attn_oA': _L0_attn_in['oA'], 'L0_attn_oB': _L0_attn_in['oB'], 'L0_ffn_router_w': _L0_ffn_in['router_w'], 'L0_ffn_router_b': _L0_ffn_in['router_b'], 'L0_ffn_w1': _L0_ffn_in['w1'], 'L0_ffn_b1': _L0_ffn_in['b1'], 'L0_ffn_w2': _L0_ffn_in['w2'], 'L0_ffn_b2': _L0_ffn_in['b2'], 'L0_ffn_sw1': _L0_ffn_in['sw1'], 'L0_ffn_sb1': _L0_ffn_in['sb1'], 'L0_ffn_sw2': _L0_ffn_in['sw2'], 'L0_ffn_sb2': _L0_ffn_in['sb2']}
    _x0 = _d['L0_attn_x']
    _d['L0_attn_x'] = jax.random.normal(jax.random.fold_in(jax.random.key(seed), 1), (16, 512, 128), dtype=_x0.dtype)
    del _x0
    return _d

def reference(L0_attn_x, L0_attn_Wq, L0_attn_Wk, L0_attn_Wv, L0_attn_Wo, L0_attn_qA, L0_attn_qB, L0_attn_kA, L0_attn_kB, L0_attn_vA, L0_attn_vB, L0_attn_oA, L0_attn_oB, L0_ffn_router_w, L0_ffn_router_b, L0_ffn_w1, L0_ffn_b1, L0_ffn_w2, L0_ffn_b2, L0_ffn_sw1, L0_ffn_sb1, L0_ffn_sw2, L0_ffn_sb2):

    def _L0_attn_ref(x, Wq, Wk, Wv, Wo, qA, qB, kA, kB, vA, vB, oA, oB):
        import jax, jax.numpy as jnp
        import numpy as np
        B, S, H = (2, 256, 128)
        NQ, NKV, HD, RANK = (16, 4, 64, 8)
        THETA = 10000.0
        LORA_SCALE = 16 / RANK
        ATTN_SCALE = 1.0 / np.sqrt(HD)

        def _lora_proj(x, W, A, Bm):
            return x @ W.T + x @ A.T @ Bm.T * LORA_SCALE

        def _rope(x, cos_h, sin_h):
            x1, x2 = (x[..., ::2], x[..., 1::2])
            return jnp.concatenate([x1 * cos_h - x2 * sin_h, x1 * sin_h + x2 * cos_h], axis=-1)

        def _forward(x, Wq, Wk, Wv, Wo, qA, qB, kA, kB, vA, vB, oA, oB):
            b, s, _ = x.shape
            q = _lora_proj(x, Wq, qA, qB).reshape(b, s, NQ, HD).transpose(0, 2, 1, 3)
            k = _lora_proj(x, Wk, kA, kB).reshape(b, s, NKV, HD).transpose(0, 2, 1, 3)
            v = _lora_proj(x, Wv, vA, vB).reshape(b, s, NKV, HD).transpose(0, 2, 1, 3)
            inv_freq = 1.0 / THETA ** (jnp.arange(0, HD, 2, dtype=jnp.float32) / HD)
            freqs = jnp.arange(s, dtype=jnp.float32)[:, None] * inv_freq[None, :]
            cos_h = jnp.cos(freqs)[None, None]
            sin_h = jnp.sin(freqs)[None, None]
            q = _rope(q, cos_h, sin_h)
            k = _rope(k, cos_h, sin_h)
            rep = NQ // NKV
            k = jnp.repeat(k, rep, axis=1)
            v = jnp.repeat(v, rep, axis=1)
            attn = jax.nn.softmax(jnp.einsum('bhqd,bhkd->bhqk', q, k) * ATTN_SCALE, axis=-1)
            out = jnp.einsum('bhqk,bhkd->bhqd', attn, v)
            out = out.transpose(0, 2, 1, 3).reshape(b, s, NQ * HD)
            return _lora_proj(out, Wo, oA, oB)
        return _forward(x, Wq, Wk, Wv, Wo, qA, qB, kA, kB, vA, vB, oA, oB)

    def _L0_ffn_ref(x, router_w, router_b, w1, b1, w2, b2, sw1, sb1, sw2, sb2):
        import jax, jax.numpy as jnp
        import numpy as np
        B, S, D = (4, 64, 128)
        E, K, H = (64, 8, 32)
        ES, HS = (2, 256)
        b_, s_, d_ = x.shape
        xf = x.reshape(-1, d_)
        probs = jax.nn.softmax(xf @ router_w + router_b, axis=-1)
        tw, ti = jax.lax.top_k(probs, K)
        tw = tw / jnp.sum(tw, axis=-1, keepdims=True)

        def body(acc, p):
            W1, B1, W2, B2, e = p
            h = jax.nn.silu(xf @ W1 + B1) @ W2 + B2
            cw = jnp.sum(jnp.where(ti == e, tw, 0.0), axis=-1)
            return (acc + cw[:, None] * h, None)
        routed, _ = jax.lax.scan(body, jnp.zeros_like(xf), (w1, b1, w2, b2, jnp.arange(w1.shape[0])))

        def shared_mlp(W1, B1, W2, B2):
            return jax.nn.silu(xf @ W1 + B1) @ W2 + B2
        shared = jnp.sum(jax.vmap(shared_mlp)(sw1, sb1, sw2, sb2), axis=0)
        return (routed + shared).reshape(b_, s_, d_)
    x = L0_attn_x
    x = x + _layernorm(_L0_attn_ref(_layernorm(x, axis=-1), L0_attn_Wq, L0_attn_Wk, L0_attn_Wv, L0_attn_Wo, L0_attn_qA, L0_attn_qB, L0_attn_kA, L0_attn_kB, L0_attn_vA, L0_attn_vB, L0_attn_oA, L0_attn_oB), axis=-1)
    x = x + _layernorm(_L0_ffn_ref(_layernorm(x, axis=-1), L0_ffn_router_w, L0_ffn_router_b, L0_ffn_w1, L0_ffn_b1, L0_ffn_w2, L0_ffn_b2, L0_ffn_sw1, L0_ffn_sb1, L0_ffn_sw2, L0_ffn_sb2), axis=-1)
    return x

_drawn_inputs = setup_inputs


def setup_inputs(seed=0):
    import zlib

    import numpy as np

    out = dict(_drawn_inputs(seed))
    spreads = {'L0_ffn_router_b': (0.0, 0.1),
     'L0_ffn_b1': (0.0, 0.8),
     'L0_ffn_b2': (0.0, 0.1),
     'L0_ffn_sb1': (0.0, 0.1),
     'L0_ffn_sb2': (0.0, 0.1)}
    factors = {'L0_ffn_w1': 3.416, 'L0_ffn_w2': 3.12}
    for name, (base, spread) in spreads.items():
        noise = np.random.default_rng([zlib.crc32(name.encode()), seed]).standard_normal(out[name].shape)
        drawn = base * np.exp(spread * noise) if base else spread * noise
        out[name] = jnp.asarray(drawn.astype(out[name].dtype))
    for name, factor in factors.items():
        out[name] = (out[name] * factor).astype(out[name].dtype)
    return out
```

```python
from contextlib import ExitStack

import concourse.bass as bass
from concourse import mybir

F32 = mybir.dt.float32
F32R = mybir.dt.float32r
ALU = mybir.AluOpType
ACT = mybir.ActivationFunctionType
AX_X = mybir.AxisListType.X

P = 128
NQ, NKV, HD, RANK = 16, 4, 64, 8
HALF = HD // 2
NE, EH, TOPK = 64, 32, 8
ES, HS = 2, 256
EPS = 1e-5
LORA_SCALE = 16 / RANK
QK_SCALE = HD ** -0.5


class Batch:

    def __init__(self, const, reg=None):
        self.const, self.reg = const, reg
        self.parity = const % 2

    def plus(self, n):
        return Batch(self.const + n, self.reg)

    def index(self):
        return self.const if self.reg is None else self.reg * 2 + self.const

    def nth(self, per_batch, k):
        base = self.const * per_batch + k
        return base if self.reg is None else self.reg * (2 * per_batch) + base

    def has(self, per_batch, k):
        return self.const * per_batch + k > 0


def attention_block(nc, ctx, args, x1_dram):
    x, Wq, Wk, Wv, Wo, qA, qB, kA, kB, vA, vB, oA, oB, cos_t, sin_t, ident_d, sel_d = args
    NB, S, D = x.shape
    TT = S // P
    UNITS = NQ * TT
    GROUPS = UNITS // 4
    PAIRS = NQ // 2
    QKV = (NQ + 2 * NKV) * HD
    OCH = QKV // P
    PROJ = TT * (QKV // 512)
    assert D == P and S == 512 and NB % 2 == 0 and NB >= 4

    def sb(name, shape, dt=F32):
        return ctx.enter_context(nc.sbuf_tensor(name, shape, dt))

    def psum(name):
        return ctx.enter_context(nc.psum_tensor(name, [P, 512], F32))

    def sem(name):
        return ctx.enter_context(nc.semaphore(name))

    q_stack = [sb(f"q_stack{i}", [P, NQ, S], F32R) for i in range(2)]
    k_stack = [sb(f"k_stack{i}", [P, NKV, 2, S], F32R) for i in range(2)]
    v_sb = [sb(f"v_sb{i}", [P, TT, NKV * HD]) for i in range(2)]
    probs = sb("probs", [P, 4, S])
    probs_t = [sb(f"probs_t{i}", [P, 2, 4, 2 * P]) for i in range(2)]
    o_t = sb("o_t", [P, PAIRS, S])
    wqkv_hi = sb("wqkv_hi", [P, QKV], F32R)
    wqkv_lo = sb("wqkv_lo", [P, QKV], F32R)
    wo_t = sb("wo_t", [P, PAIRS, D])
    x_in = sb("x_in", [P, TT, D])
    x_norm = sb("x_norm", [P, TT, D])
    xt_hi = sb("xt_hi", [P, S], F32R)
    xt_lo = sb("xt_lo", [P, S], F32R)
    rope_c = [sb(f"rope_c{i}", [P, 512]) for i in range(2)]
    rope_s = [sb(f"rope_s{i}", [P, 512]) for i in range(2)]
    cos_sb = sb("cos_sb", [P, TT, HALF])
    sin_sb = sb("sin_sb", [P, TT, HALF])
    ident = sb("ident", [P, P])
    INV_ROWS = 32 + NQ
    sel_raw = sb("sel_raw", [INV_ROWS, PAIRS * P])
    sel = sb("sel", [INV_ROWS, PAIRS * P], F32R)
    sums = [sb(f"sums{i}", [P, TT, NQ]) for i in range(2)]
    neg_max = sb("neg_max", [P, 4])
    inv_sum = sb("inv_sum", [P, TT, NQ])
    inv_split = sb("inv_split", [INV_ROWS, S], F32R)
    y_t = sb("y_t", [P, S])
    x_again = sb("x_again", [P, TT, D])
    x1 = sb("x1", [P, TT, D])
    stats = sb("stats", [P, 2, TT, 6])
    mean_var = sb("mean_var", [P, 2, TT, 2])
    rstd = sb("rstd", [P, 2, TT])
    minus_half = sb("minus_half", [P, TT])
    eps = sb("eps", [P, TT])

    raw = probs_t[0][:, :, :, :].rearrange("p a b c -> p (a b c)")
    raw2 = probs_t[1][:, :, :, :].rearrange("p a b c -> p (a b c)")
    w_raw = raw[:, 0:OCH * P].rearrange("p (o d) -> p o d", o=OCH)
    b_raw = raw[:, OCH * P:OCH * P + (OCH + 1) * RANK].rearrange("p (o r) -> p o r", o=OCH + 1)
    wo_raw = raw2[:, 0:1024]
    lora_b = o_t[0:RANK, :, :].rearrange("p a b -> p (a b)")[:, 0:(OCH + 1) * P].rearrange("p (o d) -> p o d", o=OCH + 1)
    lora_a = o_t[0:RANK, :, :].rearrange("p a b -> p (a b)")[:, 1792:1792 + 3 * P].rearrange("p (o d) -> p o d", o=3)
    oa_raw = o_t[0:RANK, :, :].rearrange("p a b -> p (a b)")[:, 2304:2304 + 1024]
    w_fold = probs[:, :, :]

    ps_scores = [psum(f"ps_scores{i}") for i in range(3)]
    ps_turned = [psum(f"ps_turned{i}") for i in range(2)]
    ps_out = psum("ps_out")
    ps_prep = psum("ps_prep")
    ps_post = psum("ps_post")

    const_loaded = sem("const_loaded")
    w_loaded = sem("w_loaded")
    set_pe = sem("set_pe")
    set_act = sem("set_act")
    set_dve = sem("set_dve")
    ready_pool = sem("ready_pool")
    scored = sem("scored")
    maxed = sem("maxed")
    exped = sem("exped")
    turned = sem("turned")
    turned_out = sem("turned_out")
    attended = sem("attended")
    o_copied = sem("o_copied")
    x_loaded = sem("x_loaded")
    prep_pe = sem("prep_pe")
    prep_free = sem("prep_free")
    prep_dve = sem("prep_dve")
    prep_stat = sem("prep_stat")
    prep_rstd = sem("prep_rstd")
    pool_chain = sem("pool_chain")
    xt_hi_done = sem("xt_hi_done")
    roped = sem("roped")
    rope_sum = sem("rope_sum")
    stacked_hi = sem("stacked_hi")
    stacked = sem("stacked")
    post_pe = sem("post_pe")
    inv_done = sem("inv_done")
    inv_hi_done = sem("inv_hi_done")
    inv_lo_done = sem("inv_lo_done")
    scaled = sem("scaled")
    projected = sem("projected")
    y_copied = sem("y_copied")
    post_stat = sem("post_stat")
    post_rstd = sem("post_rstd")
    x_again_loaded = sem("x_again_loaded")
    post_dve = sem("post_dve")
    x1_done = sem("x1_done")
    x1_stored = sem("x1_stored")

    def unit(u):
        g = u // 4
        pair, half = g // 2, g % 2
        qt = 2 * half + u % 4 // 2
        return pair * 2 + u % 2, qt

    def bank_of(u):
        return 1 if u == UNITS - 1 else u % 3

    def before_in_bank(u):
        return {0: -4, 1: -1, 2: -2, UNITS - 1: UNITS - 3}.get(u, u - 3)

    jobs = [("proj", 0)]
    for n in range(PROJ):
        if n + 1 < PROJ:
            jobs.append(("proj", n + 1))
        jobs.append(("turn", n))
    job_at = {12 + 2 * j: (j, job) for j, job in enumerate(jobs)}
    JOBS = len(jobs)
    job_of = {job: j for j, job in enumerate(jobs)}
    assert max(job_at) < UNITS - 4
    PREP_PE = 1 + JOBS

    ATTEND_AT = {1: (0,), 2: (1,), 3: (2, 3)}

    POST_INV, POST_SCALE = 2, 3
    POST_PROJ = POST_SCALE + PAIRS
    POST_Y = POST_PROJ + PAIRS
    PER_POST_PE = 1 + PAIRS + 1

    def lora_of(o):
        return 0 if o < 8 else 1 if o < 10 else 2

    x_tiles = x.rearrange("b (t p) d -> p (b t) d", p=P)
    x1_tiles = x1_dram.rearrange("b (t p) d -> p (b t) d", p=P)
    block = ctx.enter_context(nc.Block())

    def slots(eng, slot):
        slot(Batch(0), first=True, left=NB - 1)
        slot(Batch(1), left=NB - 2)
        if NB > 4:
            with eng.Fori(0, NB // 2 - 2) as i:
                slot(Batch(2, i), left=2)
                slot(Batch(3, i), left=2)
        slot(Batch(NB - 2), left=1)
        slot(Batch(NB - 1), left=0)

    @block.sync
    def _(sp):
        sp.dma_start(ident[:], ident_d).then_inc(const_loaded, 16)
        sp.dma_start(x_in[:], x_tiles[:, 0:TT, :]).then_inc(x_loaded, 16)
        sp.dma_start(b_raw[:, 0:8, :], qB.rearrange("(o p) r -> p o r", p=P)).then_inc(w_loaded, 16)
        sp.dma_start(b_raw[:, 8:10, :], kB.rearrange("(o p) r -> p o r", p=P)).then_inc(w_loaded, 16)
        sp.dma_start(b_raw[:, 10:12, :], vB.rearrange("(o p) r -> p o r", p=P)).then_inc(w_loaded, 16)
        sp.dma_start(b_raw[:, 12, :], oB).then_inc(w_loaded, 16)
        for n, a in enumerate((qA, kA, vA)):
            sp.dma_start(lora_a[:, n, :], a).then_inc(w_loaded, 16)
        sp.dma_start(oa_raw, oA).then_inc(w_loaded, 16)
        sp.dma_start(w_raw[:, 0:8, :], Wq.rearrange("(o p) d -> p o d", p=P)).then_inc(w_loaded, 16)
        sp.dma_start(w_raw[:, 8:10, :], Wk.rearrange("(o p) d -> p o d", p=P)).then_inc(w_loaded, 16)
        sp.dma_start(w_raw[:, 10:12, :], Wv.rearrange("(o p) d -> p o d", p=P)).then_inc(w_loaded, 16)
        sp.dma_start(wo_raw, Wo).then_inc(w_loaded, 16)
        sp.dma_start(cos_sb[:], cos_t).then_inc(const_loaded, 16)
        sp.dma_start(sin_sb[:], sin_t).then_inc(const_loaded, 16)
        sp.dma_start(sel_raw[:], sel_d).then_inc(const_loaded, 16)

        def load_x(c):
            sp.wait_ge(prep_dve, c.nth(1, 0))
            sp.dma_start(x_in[:], x_tiles[:, bass.ds(c.index() * TT, TT), :]).then_inc(x_loaded, 16)

        def store_x1(a):
            sp.wait_ge(x1_done, a.nth(1, 1))
            sp.dma_start(x1_tiles[:, bass.ds(a.index() * TT, TT), :], x1[:]).then_inc(x1_stored, 16)

        def load_x_again(a):
            if a.has(1, 0):
                sp.wait_ge(x1_done, a.nth(1, 0))
            sp.dma_start(x_again[:], x_tiles[:, bass.ds(a.index() * TT, TT), :]).then_inc(x_again_loaded, 16)

        def slot(b, left=0, first=False):
            if left >= 2:
                load_x(b.plus(2))
            if not first:
                load_x_again(b.plus(-1))
                store_x1(b.plus(-1))

        load_x(Batch(1))
        slots(sp, slot)
        load_x_again(Batch(NB - 1))
        store_x1(Batch(NB - 1))
        sp.wait_ge(x1_stored, 16 * NB)


    @block.gpsimd
    def _(pool):
        nc.gpsimd.memset(minus_half[:], -0.5)
        nc.gpsimd.memset(eps[:], EPS).then_inc(ready_pool, 1)
        pool.wait_ge(ready_pool, 1)

        def rstd_of(which, b, stat, done, chain_value):
            pool.wait_ge(stat, b.nth(1, 1))
            nc.gpsimd.tensor_tensor(rstd[:, which, :], mean_var[:, which, :, 1], eps[:], ALU.add).then_inc(pool_chain, 1)
            pool.wait_ge(pool_chain, chain_value)
            nc.gpsimd.tensor_tensor(rstd[:, which, :], rstd[:, which, :], minus_half[:], ALU.pow).then_inc(done, 1)

        def rotate(c, n):
            heads = 8 if n % 3 < 2 else NKV
            c4 = rope_c[n % 2][:, 0:heads * HD].rearrange("p (h e i) -> p h e i", e=2, i=HALF)
            s4 = rope_s[n % 2][:, 0:heads * HD].rearrange("p (h e i) -> p h e i", e=2, i=HALF)
            pool.wait_ge(roped, c.nth(PROJ, n + 1))
            nc.gpsimd.tensor_tensor(c4[:, :, 0, :], c4[:, :, 0, :], s4[:, :, 1, :], ALU.subtract)
            nc.gpsimd.tensor_tensor(c4[:, :, 1, :], c4[:, :, 1, :], s4[:, :, 0, :], ALU.add).then_inc(rope_sum, 1)

        def slot(b, left=0, first=False):
            if left:
                rstd_of(0, b.plus(1), prep_stat, prep_rstd, 2 if first else b.nth(2, 1))
            for n in range(PROJ):
                if left:
                    rotate(b.plus(1), n)
                if n == 2 and not first:
                    rstd_of(1, b.plus(-1), post_stat, post_rstd, b.nth(2, 2 if left else 1))

        rstd_of(0, Batch(0), prep_stat, prep_rstd, 1)
        for n in range(PROJ):
            rotate(Batch(0), n)
        slots(pool, slot)
        rstd_of(1, Batch(NB - 1), post_stat, post_rstd, 2 * NB)

    @block.scalar
    def _(act):
        act.wait_ge(set_pe, 1)
        nc.scalar.activation(lora_b[:, 0:4, :], ps_scores[0][0:RANK, :], ACT.Copy, scale=LORA_SCALE)
        nc.scalar.activation(lora_b[:, 4:8, :], ps_scores[1][0:RANK, :], ACT.Copy, scale=LORA_SCALE)
        nc.scalar.activation(lora_b[:, 8:12, :], ps_scores[2][0:RANK, :], ACT.Copy, scale=LORA_SCALE)
        nc.scalar.activation(lora_b[:, 12, :], ps_turned[0][0:RANK, 0:P], ACT.Copy, scale=LORA_SCALE).then_inc(set_act, 1)
        act.wait_ge(set_pe, 2)
        for n in range(3):
            for c0, c1, is_v in ((0, 512, False),) if n < 2 else ((0, 256, False), (256, 512, True)):
                src, dst = ps_scores[n][:, c0:c1], w_fold[:, n, c0:c1]
                if not is_v:
                    src = src.rearrange("p (h i e) -> p h e i", e=2, i=HALF)
                    dst = dst.rearrange("p (h e i) -> p h e i", e=2, i=HALF)
                ins = nc.scalar.activation(dst, src, ACT.Copy, scale=QK_SCALE if n < 2 else 1.0)
        ins.then_inc(set_act, 1)
        act.wait_ge(set_pe, 3)
        nc.scalar.activation(wo_t[:, 0:4, :], ps_turned[1][:].rearrange("p (c d) -> p c d", c=4), ACT.Copy)
        nc.scalar.activation(wo_t[:, 4:8, :], ps_out[:].rearrange("p (c d) -> p c d", c=4), ACT.Copy).then_inc(set_act, 1)

        def x_hi(c):
            act.wait_ge(prep_pe, c.nth(PREP_PE, 1))
            nc.scalar.activation(xt_hi[:], ps_prep[:], ACT.Copy).then_inc(xt_hi_done, 1)

        def stack_hi(c, j, n):
            tt, col = n // 3, n % 3
            cols = slice(tt * P, tt * P + P)
            act.wait_ge(prep_pe, c.nth(PREP_PE, 1 + j + 1))
            for s in range(2):
                rows = slice(s * HD, s * HD + HD)
                if col < 2:
                    src = ps_prep[rows, :].rearrange("p (h t) -> p h t", h=4)
                    last = nc.scalar.activation(q_stack[c.parity][0:HD, 8 * col + s:8 * col + 8:2, cols], src, ACT.Copy)
                else:
                    src = ps_prep[rows, 0:2 * P].rearrange("p (h t) -> p h t", h=2)
                    for d in range(2):
                        last = nc.scalar.activation(k_stack[c.parity][d * HD:d * HD + HD, s:NKV:2, 0, cols], src, ACT.Copy)
            last.then_inc(stacked_hi, 1)

        def exp(b, u):
            head, qt = unit(u)
            act.wait_ge(maxed, b.nth(UNITS, u + 1))
            if b.has(UNITS, u - 3):
                act.wait_ge(turned, b.nth(UNITS, u - 3))
            nc.scalar.activation(probs[:, u % 4, :], ps_scores[bank_of(u)][:], ACT.Exp,
                                 bias=neg_max[:, u % 4:u % 4 + 1],
                                 accum_out=sums[b.parity][:, qt, head:head + 1]).then_inc(exped, 1)

        def copy_turned(b, u):
            g = u // 4
            act.wait_ge(turned, b.nth(UNITS, u + 1))
            if u % 4 == 0 and b.has(GROUPS, g - 1):
                act.wait_ge(attended, b.nth(GROUPS, g - 1))
            qo = u % 4 // 2 * P
            nc.scalar.activation(probs_t[g % 2][:, u % 2, :, qo:qo + P],
                                 ps_turned[u % 2][:].rearrange("p (k q) -> p k q", k=4), ACT.Copy).then_inc(turned_out, 1)

        def copy_out(b, pair):
            act.wait_ge(attended, b.nth(GROUPS, 2 * pair + 2))
            if b.has(PAIRS, pair + 1 - PAIRS):
                act.wait_ge(projected, b.nth(PAIRS, pair + 1 - PAIRS))
            nc.scalar.activation(o_t[:, pair, :], ps_out[:], ACT.Copy).then_inc(o_copied, 1)

        def inverse_hi(a):
            act.wait_ge(post_pe, a.nth(PER_POST_PE, 1))
            nc.scalar.activation(inv_split[0:NQ, :], ps_post[0:NQ, :], ACT.Copy).then_inc(inv_hi_done, 1)

        def copy_y(a):
            act.wait_ge(projected, a.nth(PAIRS, PAIRS))
            nc.scalar.activation(y_t[:], ps_post[:], ACT.Copy).then_inc(y_copied, 1)

        def slot(b, left=0, first=False):
            for u in range(UNITS):
                if u % 8 == 4 and (u >= 12 or not first):
                    copy_out(b if u >= 12 else b.plus(-1), (u // 8 - 1) % PAIRS)
                if u + 2 < UNITS:
                    exp(b, u + 2)
                elif left:
                    exp(b.plus(1), u + 2 - UNITS)
                copy_turned(b, u)
                if not first and u == POST_INV:
                    inverse_hi(b.plus(-1))
                if not first and u == POST_Y:
                    copy_y(b.plus(-1))
                if left and u == 4:
                    x_hi(b.plus(1))
                if left and u in job_at:
                    j, job = job_at[u]
                    if job[0] == "turn":
                        stack_hi(b.plus(1), j, job[1])

        x_hi(Batch(0))
        for n in range(PROJ):
            stack_hi(Batch(0), job_of["turn", n], n)
        exp(Batch(0), 0)
        exp(Batch(0), 1)
        slots(act, slot)
        copy_out(Batch(NB - 1), PAIRS - 1)
        inverse_hi(Batch(NB - 1))
        copy_y(Batch(NB - 1))

    @block.vector
    def _(dve):
        dve.wait_ge(const_loaded, 64)
        nc.vector.memset(inv_split[:].bitcast(F32), 0.0)
        nc.vector.tensor_copy(sel[:], sel_raw[:]).then_inc(set_dve, 1)
        dve.wait_ge(set_act, 2)
        nc.vector.tensor_copy(wqkv_hi[:], w_fold[:, 0:3, :].rearrange("p a b -> p (a b)")).then_inc(set_dve, 1)
        dve.wait_ge(set_dve, 2)
        nc.vector.tensor_tensor(wqkv_lo[:], w_fold[:, 0:3, :].rearrange("p a b -> p (a b)"), wqkv_hi[:].bitcast(F32),
                                ALU.subtract).then_inc(set_dve, 1)

        def variance(which, src, stat):
            for t in range(TT):
                nc.vector.bn_stats(stats[:, which, t, :], src[:, t, :])
            dve.drain()
            for t in range(TT):
                last = nc.vector.bn_aggr(mean_var[:, which, t, :], stats[:, which, t, :])
            last.then_inc(stat, 1)

        def normalise(which, out, src, t):
            return nc.vector.tensor_scalar(out[:, t, :], src[:, t, :], mean_var[:, which, t, 0:1], rstd[:, which, t:t + 1],
                                           ALU.subtract, ALU.mult)

        def norm_x(c):
            dve.wait_ge(x_loaded, c.nth(16, 16))
            variance(0, x_in, prep_stat)

        def norm_x_out(c):
            dve.wait_ge(prep_rstd, c.nth(1, 1))
            if c.has(PREP_PE, 1 - PREP_PE):
                dve.wait_ge(prep_pe, c.nth(PREP_PE, 1 - PREP_PE))
            for t in range(TT):
                last = normalise(0, x_norm, x_in, t)
            last.then_inc(prep_dve, 1)

        def x_lo(c):
            dve.wait_ge(xt_hi_done, c.nth(1, 1))
            nc.vector.tensor_tensor(xt_lo[:], ps_prep[:], xt_hi[:].bitcast(F32), ALU.subtract).then_inc(prep_free, 1)

        def rope_products(c, j, n):
            tt, col, r = n // 3, n % 3, n % 2
            dve.wait_ge(prep_pe, c.nth(PREP_PE, 1 + j + 1))
            width = 512 if col < 2 else NKV * HD
            src = ps_prep[:, 0:width].rearrange("p (h i) -> p h i", i=HALF)
            cs = cos_sb[:, tt, :].unsqueeze(1).to_broadcast([P, width // HALF, HALF])
            sn = sin_sb[:, tt, :].unsqueeze(1).to_broadcast([P, width // HALF, HALF])
            nc.vector.tensor_tensor(rope_c[r][:, 0:width].rearrange("p (h i) -> p h i", i=HALF), src, cs, ALU.mult)
            if col == 2:
                if c.has(GROUPS, -GROUPS):
                    dve.wait_ge(attended, c.nth(GROUPS, -GROUPS))
                nc.vector.tensor_copy(v_sb[c.parity][:, tt, :], ps_prep[:, width:512])
            nc.vector.tensor_tensor(rope_s[r][:, 0:width].rearrange("p (h i) -> p h i", i=HALF), src, sn,
                                    ALU.mult).then_inc(roped, 1)

        def stack_lo(c, n):
            tt, col = n // 3, n % 3
            cols = slice(tt * P, tt * P + P)
            dve.wait_ge(stacked_hi, c.nth(PROJ, n + 1))
            for s in range(2):
                rows = slice(s * HD, s * HD + HD)
                if col < 2:
                    heads = q_stack[c.parity][:, 8 * col + s:8 * col + 8:2, cols]
                    src = ps_prep[rows, :].rearrange("p (h t) -> p h t", h=4)
                    last = nc.vector.tensor_tensor(heads[HD:2 * HD], src, heads[0:HD].bitcast(F32), ALU.subtract)
                else:
                    src = ps_prep[rows, 0:2 * P].rearrange("p (h t) -> p h t", h=2)
                    for d in range(2):
                        heads = k_stack[c.parity][d * HD:d * HD + HD, s:NKV:2, :, cols]
                        last = nc.vector.tensor_tensor(heads[:, :, 1, :], src, heads[:, :, 0, :].bitcast(F32), ALU.subtract)
            last.then_inc(stacked, 1)

        def do_job(c, j, job):
            if job[0] == "proj":
                rope_products(c, j, job[1])
            else:
                stack_lo(c, job[1])

        def maxima(b, u):
            dve.wait_ge(scored, b.nth(UNITS, u + 1))
            if b.has(UNITS, u - 3):
                dve.wait_ge(exped, b.nth(UNITS, u - 3))
            nc.vector.reduce_max(neg_max[:, u % 4:u % 4 + 1], ps_scores[bank_of(u)][:], AX_X, negate=True).then_inc(maxed, 1)

        def inverse(a):
            dve.wait_ge(exped, a.nth(UNITS, UNITS))
            if a.has(PER_POST_PE, 1 - PER_POST_PE):
                dve.wait_ge(post_pe, a.nth(PER_POST_PE, 1 - PER_POST_PE))
            nc.vector.reciprocal(inv_sum[:], sums[a.parity][:]).then_inc(inv_done, 1)

        def inverse_lo(a):
            dve.wait_ge(inv_hi_done, a.nth(1, 1))
            nc.vector.tensor_tensor(inv_split[32:32 + NQ, :], ps_post[0:NQ, :], inv_split[0:NQ, :].bitcast(F32), ALU.subtract).then_inc(inv_lo_done, 1)

        def scale_out(a, pair):
            dve.wait_ge(post_pe, a.nth(PER_POST_PE, 2 + pair))
            dve.wait_ge(o_copied, a.nth(PAIRS, pair + 1))
            nc.vector.tensor_tensor(o_t[:, pair, :], o_t[:, pair, :], ps_post[:], ALU.mult).then_inc(scaled, 1)

        def y_stats(a):
            dve.wait_ge(post_pe, a.nth(PER_POST_PE, PER_POST_PE))
            variance(1, ps_post[:].rearrange("p (t d) -> p t d", t=TT), post_stat)

        def residual(a):
            dve.wait_ge(post_rstd, a.nth(1, 1))
            if a.has(16, 0):
                dve.wait_ge(x1_stored, a.nth(16, 0))
            for t in range(TT):
                last = normalise(1, x1, ps_post[:].rearrange("p (t d) -> p t d", t=TT), t)
            last.then_inc(post_dve, 1)
            dve.wait_ge(post_dve, a.nth(1, 1))
            dve.wait_ge(x_again_loaded, a.nth(16, 16))
            nc.vector.tensor_tensor(x1[:], x1[:], x_again[:], ALU.add).then_inc(x1_done, 1)

        def slot(b, left=0, first=False):
            for u in range(UNITS):
                if u + 3 < UNITS:
                    maxima(b, u + 3)
                elif left:
                    maxima(b.plus(1), u + 3 - UNITS)
                if left and u == 0:
                    norm_x(b.plus(1))
                if left and u == 2:
                    norm_x_out(b.plus(1))
                if left and u == 4:
                    x_lo(b.plus(1))
                if left and u in job_at:
                    do_job(b.plus(1), *job_at[u])
                if not first:
                    a = b.plus(-1)
                    if u == 0:
                        inverse(a)
                    if u == POST_INV:
                        inverse_lo(a)
                    if POST_SCALE <= u < POST_SCALE + PAIRS:
                        scale_out(a, u - POST_SCALE)
                    if u == POST_Y + 1:
                        y_stats(a)
                    if u == POST_Y + 6:
                        residual(a)

        c = Batch(0)
        norm_x(c)
        norm_x_out(c)
        x_lo(c)
        for j, job in enumerate(jobs):
            do_job(c, j, job)
        for u in range(3):
            maxima(c, u)
        slots(dve, slot)
        a = Batch(NB - 1)
        inverse(a)
        inverse_lo(a)
        for pair in range(PAIRS):
            scale_out(a, pair)
        y_stats(a)
        residual(a)

    @block.tensor
    def _(pe):
        mm, turn = nc.tensor.matmul, nc.tensor.transpose
        pe.wait_ge(const_loaded, 64)
        pe.wait_ge(w_loaded, 12 * 16)
        for o in range(OCH):
            turn(ps_scores[o // 4][0:RANK, o % 4 * P:(o % 4 + 1) * P], b_raw[:, o, :], ident[:])
        turn(ps_turned[0][0:RANK, 0:P], b_raw[:, OCH, :], ident[:]).then_inc(set_pe, 1)
        pe.wait_ge(set_act, 1)
        for o in range(OCH):
            out = ps_scores[o // 4][:, o % 4 * P:(o % 4 + 1) * P]
            mm(out, w_raw[:, o, :], ident[:], start=True, stop=False)
            last = mm(out, lora_a[:, lora_of(o), :], lora_b[:, o, :], start=False, stop=True)
        last.then_inc(set_pe, 1)
        for o in range(PAIRS):
            out = (ps_turned[1], ps_out)[o // 4][:, o % 4 * P:(o % 4 + 1) * P]
            mm(out, wo_raw[:, o * P:(o + 1) * P], ident[:], start=True, stop=False)
            last = mm(out, oa_raw[:, o * P:(o + 1) * P], lora_b[:, OCH, :], start=False, stop=True)
        last.then_inc(set_pe, 1)
        pe.wait_ge(set_dve, 3)
        pe.wait_ge(set_act, 3)

        def turn_x(c):
            pe.wait_ge(prep_dve, c.nth(1, 1))
            if c.has(PREP_PE, 0):
                pe.wait_ge(stacked, c.nth(PROJ, 0))
            for t in range(TT):
                last = turn(ps_prep[:, t * P:(t + 1) * P], x_norm[:, t, :], ident[:])
            last.then_inc(prep_pe, 1)

        def wait_prep_free(c, j):
            if j == 0:
                pe.wait_ge(prep_free, c.nth(1, 1))
            elif jobs[j - 1][0] == "proj":
                pe.wait_ge(roped, c.nth(PROJ, jobs[j - 1][1] + 1))
            else:
                pe.wait_ge(stacked, c.nth(PROJ, jobs[j - 1][1] + 1))

        def do_job(c, j, job):
            wait_prep_free(c, j)
            n = job[1]
            tt, col = n // 3, n % 3
            if job[0] == "proj":
                rows, cols = slice(tt * P, tt * P + P), slice(col * 512, col * 512 + 512)
                mm(ps_prep[:], xt_hi[:, rows], wqkv_hi[:, cols], start=True, stop=False)
                mm(ps_prep[:], xt_hi[:, rows], wqkv_lo[:, cols], start=False, stop=False)
                mm(ps_prep[:], xt_lo[:, rows], wqkv_hi[:, cols], start=False, stop=True).then_inc(prep_pe, 1)
            else:
                pe.wait_ge(rope_sum, c.nth(PROJ, n + 1))
                for h in range(4 if col < 2 else 2):
                    last = turn(ps_prep[:, h * P:(h + 1) * P], rope_c[n % 2][:, h * P:(h + 1) * P], ident[:])
                last.then_inc(prep_pe, 1)

        def scores(b, u):
            head, qt = unit(u)
            if u == 0:
                pe.wait_ge(stacked, b.nth(PROJ, PROJ))
            before = before_in_bank(u) + 1
            if b.has(UNITS, before):
                pe.wait_ge(exped, b.nth(UNITS, before))
            out = ps_scores[bank_of(u)]
            q = q_stack[b.parity][:, head, qt * P:(qt + 1) * P]
            mm(out[:], q, k_stack[b.parity][:, head // 4, 0, :], start=True, stop=False)
            mm(out[:], q, k_stack[b.parity][:, head // 4, 1, :], start=False, stop=True).then_inc(scored, 1)

        def turn_probs(b, u):
            pe.wait_ge(exped, b.nth(UNITS, u + 1))
            if b.has(UNITS, u - 1):
                pe.wait_ge(turned_out, b.nth(UNITS, u - 1))
            for k in range(4):
                last = turn(ps_turned[u % 2][:, k * P:(k + 1) * P], probs[:, u % 4, k * P:(k + 1) * P], ident[:])
            last.then_inc(turned, 1)

        def attend(b, g, k):
            pair, half = g // 2, g % 2
            if k == 0:
                pe.wait_ge(turned_out, b.nth(UNITS, 4 * g + 4))
                if half == 0 and b.has(PAIRS, pair):
                    pe.wait_ge(o_copied, b.nth(PAIRS, pair))
            for j in range(2):
                kv = (2 * pair + j) // 4
                last = mm(ps_out[HD * j:HD * j + HD, half * 256:half * 256 + 256],
                          v_sb[b.parity][:, k, kv * HD:(kv + 1) * HD], probs_t[g % 2][:, j, k, :],
                          start=(k == 0), stop=(k == 3))
            if k == 3:
                last.then_inc(attended, 1)

        def inverse_rows(a):
            pe.wait_ge(inv_done, a.nth(1, 1))
            if a.has(1, 0):
                pe.wait_ge(post_dve, a.nth(1, 0))
            for t in range(TT):
                last = turn(ps_post[0:NQ, t * P:(t + 1) * P], inv_sum[:, t, :], ident[:])
            last.then_inc(post_pe, 1)

        def spread_inverse(a, pair):
            if pair == 0:
                pe.wait_ge(inv_lo_done, a.nth(1, 1))
            else:
                pe.wait_ge(scaled, a.nth(PAIRS, pair))
            mm(ps_post[:], sel[:, pair * P:(pair + 1) * P], inv_split[:], start=True, stop=True).then_inc(post_pe, 1)

        def project(a, pair):
            pe.wait_ge(scaled, a.nth(PAIRS, PAIRS))
            mm(ps_post[:], wo_t[:, pair, :], o_t[:, pair, :], start=(pair == 0), stop=(pair == PAIRS - 1)).then_inc(projected, 1)

        def turn_y(a):
            pe.wait_ge(y_copied, a.nth(1, 1))
            for t in range(TT):
                last = turn(ps_post[:, t * P:(t + 1) * P], y_t[:, t * P:(t + 1) * P], ident[:])
            last.then_inc(post_pe, 1)

        def slot(b, left=0, first=False):
            for u in range(UNITS):
                turn_probs(b, u)
                if u + 3 < UNITS:
                    scores(b, u + 3)
                elif left:
                    scores(b.plus(1), u + 3 - UNITS)
                if u >= 4 or not first:
                    for k in ATTEND_AT.get(u % 4, ()):
                        attend(b if u >= 4 else b.plus(-1), (u // 4 - 1) % GROUPS, k)
                if left and u == 3:
                    turn_x(b.plus(1))
                if left and u in job_at:
                    do_job(b.plus(1), *job_at[u])
                if not first:
                    a = b.plus(-1)
                    if u == POST_INV - 1:
                        inverse_rows(a)
                    if POST_SCALE <= u < POST_SCALE + PAIRS:
                        spread_inverse(a, u - POST_SCALE)
                    if POST_PROJ <= u < POST_PROJ + PAIRS:
                        project(a, u - POST_PROJ)
                    if u == POST_Y + 1:
                        turn_y(a)

        c = Batch(0)
        turn_x(c)
        for j, job in enumerate(jobs):
            do_job(c, j, job)
        for u in range(3):
            scores(c, u)
        slots(pe, slot)
        a = Batch(NB - 1)
        for k in range(4):
            attend(a, GROUPS - 1, k)
        inverse_rows(a)
        for pair in range(PAIRS):
            spread_inverse(a, pair)
        for pair in range(PAIRS):
            project(a, pair)
        turn_y(a)


def experts_block(nc, ctx, args, x1_dram, out):
    router_w, router_b, w1, b1, w2, b2, sw1, sb1, sw2, sb2, ident_d = args
    NB, S, D = x1_dram.shape
    TT = S // P
    EC = NE * EH // P
    EPC = P // EH
    SC = ES * HS // P
    CHUNKS = EC + SC
    assert D == P and CHUNKS % 4 == 0

    def sb(name, shape, dt=F32):
        return ctx.enter_context(nc.sbuf_tensor(name, shape, dt))

    def psum(name):
        return ctx.enter_context(nc.psum_tensor(name, [P, 512], F32))

    def sem(name):
        return ctx.enter_context(nc.semaphore(name))

    w1_sb = sb("w1_sb", [P, CHUNKS * P])
    w1_hi = sb("w1_hi", [P, CHUNKS * P], F32R)
    w1_lo = sb("w1_lo", [P, CHUNKS * P], F32R)
    w2_sb = sb("w2_sb", [P, CHUNKS, D])
    bias_rows = sb("bias_rows", [CHUNKS + ES, P])
    bias_cols = sb("bias_cols", [P, CHUNKS + ES])
    sb2_sum = sb("sb2_sum", [P, 1])
    b2_sb = sb("b2_sb", [P, D])
    b2_hi = sb("b2_hi", [P, D], F32R)
    b2_lo = sb("b2_lo", [P, D], F32R)
    router_sb = sb("router_sb", [P, NE])
    router_bias = sb("router_bias", [P, NE])
    spread_raw = sb("spread_raw", [P, EC * P])
    spread = sb("spread", [P, EC * P], F32R)
    ident2 = sb("ident2", [P, P])
    xe_in = sb("xe_in", [P, TT, D])
    xe_norm = sb("xe_norm", [P, TT, D])
    xe_t = sb("xe_t", [P, S])
    xe_hi = [sb(f"xe_hi{i}", [P, S], F32R) for i in range(2)]
    xe_lo = [sb(f"xe_lo{i}", [P, S], F32R) for i in range(2)]
    weight_t = [sb(f"weight_t{i}", [P, S], F32R) for i in range(2)]
    hidden = sb("hidden", [P, 4, S])
    gated = sb("gated", [P, 4, S])
    logits = sb("logits", [P, TT, NE])
    expo = sb("expo", [P, TT, NE])
    chosen = sb("chosen", [P, TT, NE])
    weights = sb("weights", [P, TT, NE])
    weight_split = sb("weight_split", [P, TT, 2, NE])
    top8 = sb("top8", [P, TT, TOPK])
    small = sb("small", [P, 5, TT])
    ye_t = sb("ye_t", [P, S])
    xe_again = sb("xe_again", [P, TT, D])
    out_sb = sb("out_sb", [P, TT, D])
    stats = sb("stats2", [P, 2, TT, 6])
    mean_var = sb("mean_var2", [P, 2, TT, 2])
    rstd = sb("rstd2", [P, 2, TT])
    minus_half = sb("minus_half2", [P, TT])
    eps = sb("eps2", [P, TT])

    ps_hidden = [psum(f"ps_hidden{i}") for i in range(2)]
    ps_weight = [psum(f"ps_weight{i}") for i in range(2)]
    ps_y = [psum(f"ps_y{i}") for i in range(2)]
    ps_prep = psum("ps_prep2")
    ps_post = psum("ps_post2")

    loaded_small = sem("loaded_small")
    loaded_w1 = sem("loaded_w1")
    loaded_w2 = sem("loaded_w2")
    set_pool = sem("set_pool")
    set_pe2 = sem("set_pe2")
    set_act2 = sem("set_act2")
    set_dve2 = sem("set_dve2")
    xe_loaded = sem("xe_loaded")
    norm_dve = sem("norm_dve")
    norm_stat = sem("norm_stat")
    norm_rstd = sem("norm_rstd")
    pool_chain2 = sem("pool_chain2")
    prep_pe2 = sem("prep_pe2")
    xe_copied = sem("xe_copied")
    split_dve = sem("split_dve")
    route_dve = sem("route_dve")
    route_exp = sem("route_exp")
    weight_ready = sem("weight_ready")
    up_done = sem("up_done")
    activated = sem("activated")
    weighted = sem("weighted")
    down_done = sem("down_done")
    ye_copied = sem("ye_copied")
    post_pe2 = sem("post_pe2")
    post_stat2 = sem("post_stat2")
    post_rstd2 = sem("post_rstd2")
    post_dve2 = sem("post_dve2")
    xe_again_loaded = sem("xe_again_loaded")
    out_done = sem("out_done")
    out_stored = sem("out_stored")

    N_STATS, N_OUT, N_TURN, N_SPLIT, R_LOGITS, R_SHIFT, R_EXP = 0, 1, 2, 3, 4, 5, 6
    R_PROBS, R_TOP, R_MATCH, R_PICK, R_WEIGH, R_LO, R_TURN, R_COPY = 8, 9, 10, 11, 12, 13, 14, 15
    Y_TURN, Y_STATS, Y_OUT = 1, 2, 5
    PREP_PE = 3
    ROUTE = 11

    x1_tiles = x1_dram.rearrange("b (t p) d -> p (b t) d", p=P)
    out_tiles = out.rearrange("b (t p) d -> p (b t) d", p=P)
    block = ctx.enter_context(nc.Block())

    def slots(eng, slot):
        slot(Batch(0), first=True, left=NB - 1)
        slot(Batch(1), left=NB - 2)
        if NB > 4:
            with eng.Fori(0, NB // 2 - 2) as i:
                slot(Batch(2, i), left=2)
                slot(Batch(3, i), left=2)
        slot(Batch(NB - 2), left=1)
        slot(Batch(NB - 1), left=0)

    @block.sync
    def _(sp):
        sp.dma_start(xe_in[:], x1_tiles[:, 0:TT, :]).then_inc(xe_loaded, 16)
        sp.dma_start(ident2[:], ident_d).then_inc(loaded_small, 16)
        sp.dma_start(router_sb[:], router_w).then_inc(loaded_small, 16)
        sp.dma_start(router_bias[:], router_b.partition_broadcast(P)).then_inc(loaded_small, 16)
        sp.dma_start(bias_rows[0:EC, :], b1.rearrange("(c e) h -> c (e h)", e=EPC)).then_inc(loaded_small, 16)
        sp.dma_start(bias_rows[EC:CHUNKS, :], sb1.rearrange("e (c h) -> (e c) h", h=P)).then_inc(loaded_small, 16)
        sp.dma_start(bias_rows[CHUNKS:CHUNKS + ES, :], sb2).then_inc(loaded_small, 16)
        sp.dma_start(b2_sb[0:NE, :], b2).then_inc(loaded_small, 16)
        sp.dma_start(b2_sb[NE:2 * NE, :], b2).then_inc(loaded_small, 16)
        sp.dma_start(w1_sb[:, 0:EC * P].rearrange("d (e h) -> d e h", e=NE), w1.rearrange("e d h -> d e h")).then_inc(loaded_w1, 16)
        sp.dma_start(w1_sb[:, EC * P:CHUNKS * P].rearrange("d (e h) -> d e h", e=ES), sw1.rearrange("e d h -> d e h")).then_inc(loaded_w1, 16)
        sp.dma_start(w2_sb[:, 0:EC, :], w2.rearrange("(c e) h d -> (e h) c d", e=EPC)).then_inc(loaded_w2, 16)
        sp.dma_start(w2_sb[:, EC:CHUNKS, :], sw2.rearrange("e (c h) d -> h (e c) d", h=P)).then_inc(loaded_w2, 16)

        def load_x1(c):
            sp.wait_ge(norm_dve, c.nth(1, 0))
            sp.dma_start(xe_in[:], x1_tiles[:, bass.ds(c.index() * TT, TT), :]).then_inc(xe_loaded, 16)

        def load_again(a):
            if a.has(1, 0):
                sp.wait_ge(out_done, a.nth(1, 0))
            sp.dma_start(xe_again[:], x1_tiles[:, bass.ds(a.index() * TT, TT), :]).then_inc(xe_again_loaded, 16)

        def store(a):
            sp.wait_ge(out_done, a.nth(1, 1))
            sp.dma_start(out_tiles[:, bass.ds(a.index() * TT, TT), :], out_sb[:]).then_inc(out_stored, 16)

        def slot(b, left=0, first=False):
            if left >= 2:
                load_x1(b.plus(2))
            if not first:
                load_again(b.plus(-1))
                store(b.plus(-1))

        load_x1(Batch(1))
        slots(sp, slot)
        load_again(Batch(NB - 1))
        store(Batch(NB - 1))
        sp.wait_ge(out_stored, 16 * NB)

    @block.gpsimd
    def _(pool):
        nc.gpsimd.memset(minus_half[:], -0.5)
        nc.gpsimd.memset(eps[:], EPS)
        nc.gpsimd.memset(spread_raw[:], 0.0).then_inc(set_pool, 1)
        pool.wait_ge(set_pool, 1)
        view = spread_raw[:].rearrange("p (c e h) -> p c e h", c=EC, e=EPC)
        for half in range(2):
            nc.gpsimd.affine_select(out=view, in_=view, compare_op=ALU.not_equal, fill=1.0, base=-half * NE,
                                    pattern=[[-EPC, EC], [-1, EPC], [0, EH]], channel_multiplier=1).then_inc(set_pool, 1)
            pool.wait_ge(set_pool, 2 + half)

        def rstd_of(which, b, stat, done, chain_value):
            pool.wait_ge(stat, b.nth(1, 1))
            nc.gpsimd.tensor_tensor(rstd[:, which, :], mean_var[:, which, :, 1], eps[:], ALU.add).then_inc(pool_chain2, 1)
            pool.wait_ge(pool_chain2, chain_value)
            nc.gpsimd.tensor_tensor(rstd[:, which, :], rstd[:, which, :], minus_half[:], ALU.pow).then_inc(done, 1)

        def slot(b, left=0, first=False):
            if left:
                rstd_of(0, b.plus(1), norm_stat, norm_rstd, 2 if first else b.nth(2, 1))
            if not first:
                rstd_of(1, b.plus(-1), post_stat2, post_rstd2, b.nth(2, 2 if left else 1))

        rstd_of(0, Batch(0), norm_stat, norm_rstd, 1)
        slots(pool, slot)
        rstd_of(1, Batch(NB - 1), post_stat2, post_rstd2, 2 * NB)

    @block.scalar
    def _(act):
        act.wait_ge(set_pe2, 1)
        nc.scalar.activation(bias_cols[:], ps_post[:, 0:CHUNKS + ES], ACT.Copy).then_inc(set_act2, 1)
        act.wait_ge(set_act2, 1)
        act.wait_ge(set_dve2, 1)

        def copy_x(c):
            act.wait_ge(prep_pe2, c.nth(PREP_PE, 1))
            if c.has(2, 0):
                act.wait_ge(split_dve, c.nth(2, 0))
            nc.scalar.activation(xe_t[:], ps_prep[:], ACT.Copy).then_inc(xe_copied, 1)

        def activate(b, c):
            act.wait_ge(up_done, b.nth(CHUNKS, c + 1))
            if c < EC:
                if b.has(EC, max(c - 3, 0)):
                    act.wait_ge(weighted, b.nth(EC, max(c - 3, 0)))
                dst = hidden
            else:
                act.wait_ge(down_done, b.nth(CHUNKS, c - 3))
                dst = gated
            nc.scalar.activation(dst[:, c % 4, :], ps_hidden[c % 2][:], ACT.Silu, bias=bias_cols[:, c:c + 1]).then_inc(activated, 1)

        def exponentials(c):
            act.wait_ge(route_dve, c.nth(ROUTE, 3))
            nc.scalar.activation(expo[:], logits[:], ACT.Exp).then_inc(route_exp, 1)

        def copy_y(b):
            act.wait_ge(down_done, b.nth(CHUNKS, CHUNKS))
            if b.has(1, 0):
                act.wait_ge(post_pe2, b.nth(1, 0))
            nc.scalar.activation(ye_t[:], ps_y[b.parity][:], ACT.Identity, bias=sb2_sum[:, 0:1]).then_inc(ye_copied, 1)

        def slot(b, left=0, first=False):
            for c in range(CHUNKS):
                if not first and c == 0:
                    copy_y(b.plus(-1))
                if c + 2 < CHUNKS:
                    activate(b, c + 2)
                elif left:
                    activate(b.plus(1), c + 2 - CHUNKS)
                if left and c == N_TURN:
                    copy_x(b.plus(1))
                if left and c == R_EXP:
                    exponentials(b.plus(1))

        copy_x(Batch(0))
        exponentials(Batch(0))
        activate(Batch(0), 0)
        activate(Batch(0), 1)
        slots(act, slot)
        copy_y(Batch(NB - 1))

    @block.vector
    def _(dve):
        def variance(which, src, stat):
            for t in range(TT):
                nc.vector.bn_stats(stats[:, which, t, :], src[:, t, :])
            dve.drain()
            for t in range(TT):
                last = nc.vector.bn_aggr(mean_var[:, which, t, :], stats[:, which, t, :])
            last.then_inc(stat, 1)

        def normalise(which, out, src, t):
            return nc.vector.tensor_scalar(out[:, t, :], src[:, t, :], mean_var[:, which, t, 0:1], rstd[:, which, t:t + 1],
                                           ALU.subtract, ALU.mult)

        def norm_x(c):
            dve.wait_ge(xe_loaded, c.nth(16, 16))
            variance(0, xe_in, norm_stat)

        def norm_out(c):
            dve.wait_ge(norm_rstd, c.nth(1, 1))
            if c.has(PREP_PE, 1 - PREP_PE):
                dve.wait_ge(prep_pe2, c.nth(PREP_PE, 1 - PREP_PE))
            for t in range(TT):
                last = normalise(0, xe_norm, xe_in, t)
            last.then_inc(norm_dve, 1)

        def split_x(c):
            dve.wait_ge(xe_copied, c.nth(1, 1))
            if c.has(CHUNKS, -CHUNKS):
                dve.wait_ge(up_done, c.nth(CHUNKS, -CHUNKS))
            nc.vector.tensor_copy(xe_hi[c.parity][:], xe_t[:]).then_inc(split_dve, 1)
            dve.wait_ge(split_dve, c.nth(2, 1))
            nc.vector.tensor_tensor(xe_lo[c.parity][:], xe_t[:], xe_hi[c.parity][:].bitcast(F32), ALU.subtract).then_inc(split_dve, 1)

        def per_token(k):
            return small[:, k, :].unsqueeze(2).to_broadcast([P, TT, NE])

        def shift_logits(c):
            dve.wait_ge(prep_pe2, c.nth(PREP_PE, 2))
            bias = router_bias[:].unsqueeze(1).to_broadcast([P, TT, NE])
            nc.vector.tensor_tensor(logits[:], ps_prep[:, 0:TT * NE].rearrange("p (t e) -> p t e", t=TT), bias, ALU.add).then_inc(route_dve, 1)
            dve.wait_ge(route_dve, c.nth(ROUTE, 1))
            nc.vector.reduce_max(small[:, 0, :], logits[:], AX_X, negate=True).then_inc(route_dve, 1)
            dve.wait_ge(route_dve, c.nth(ROUTE, 2))
            nc.vector.tensor_tensor(logits[:], logits[:], per_token(0), ALU.add).then_inc(route_dve, 1)

        def probabilities(c):
            dve.wait_ge(route_exp, c.nth(1, 1))
            nc.vector.reduce_sum(small[:, 1, :], expo[:], AX_X).then_inc(route_dve, 1)
            dve.wait_ge(route_dve, c.nth(ROUTE, 4))
            nc.vector.reciprocal(small[:, 2, :], small[:, 1, :]).then_inc(route_dve, 1)
            dve.wait_ge(route_dve, c.nth(ROUTE, 5))
            nc.vector.tensor_tensor(expo[:], expo[:], per_token(2), ALU.mult).then_inc(route_dve, 1)

        def top(c):
            dve.drain()
            for t in range(TT):
                last = nc.vector.max(top8[:, t, :], expo[:, t, :])
            last.then_inc(route_dve, 1)

        def match(c):
            dve.wait_ge(route_dve, c.nth(ROUTE, 7))
            nc.vector.reduce_sum(small[:, 3, :], top8[:], AX_X)
            for t in range(TT):
                last = nc.vector.match_replace(chosen[:, t, :], top8[:, t, :], expo[:, t, :], -1.0)
            last.then_inc(route_dve, 1)

        def pick(c):
            dve.wait_ge(route_dve, c.nth(ROUTE, 8))
            nc.vector.scalar_tensor_tensor(weights[:], chosen[:], 0.0, expo[:], ALU.is_lt, ALU.mult)
            nc.vector.reciprocal(small[:, 4, :], small[:, 3, :]).then_inc(route_dve, 1)

        def weigh(c):
            dve.wait_ge(route_dve, c.nth(ROUTE, 9))
            nc.vector.tensor_tensor(weights[:], weights[:], per_token(4), ALU.mult).then_inc(route_dve, 1)
            dve.wait_ge(route_dve, c.nth(ROUTE, 10))
            if c.has(PREP_PE, 0):
                dve.wait_ge(prep_pe2, c.nth(PREP_PE, 0))
            nc.vector.tensor_copy(weight_split[:, :, 0, :].bitcast(F32R), weights[:]).then_inc(weight_ready, 1)

        def weigh_lo(c):
            dve.wait_ge(weight_ready, c.nth(2, 1))
            nc.vector.tensor_tensor(weight_split[:, :, 1, :], weights[:], weight_split[:, :, 0, :], ALU.subtract).then_inc(weight_ready, 1)

        def copy_weights(c):
            dve.wait_ge(prep_pe2, c.nth(PREP_PE, 3))
            if c.has(CHUNKS, -CHUNKS):
                dve.wait_ge(down_done, c.nth(CHUNKS, -CHUNKS))
            nc.vector.tensor_copy(weight_t[c.parity][:], ps_prep[:]).then_inc(route_dve, 1)

        def weigh_hidden(b, c):
            dve.wait_ge(activated, b.nth(CHUNKS, c + 1))
            dve.wait_ge(up_done, b.nth(CHUNKS, c + 1))
            if b.has(CHUNKS, c - 3):
                dve.wait_ge(down_done, b.nth(CHUNKS, c - 3))
            nc.vector.tensor_tensor(gated[:, c % 4, :], hidden[:, c % 4, :], ps_weight[c % 2][:], ALU.mult).then_inc(weighted, 1)

        def y_stats(a):
            dve.wait_ge(post_pe2, a.nth(1, 1))
            variance(1, ps_post[:].rearrange("p (t d) -> p t d", t=TT), post_stat2)

        def y_out(a):
            dve.wait_ge(post_rstd2, a.nth(1, 1))
            if a.has(16, 0):
                dve.wait_ge(out_stored, a.nth(16, 0))
            for t in range(TT):
                last = normalise(1, out_sb, ps_post[:].rearrange("p (t d) -> p t d", t=TT), t)
            last.then_inc(post_dve2, 1)
            dve.wait_ge(post_dve2, a.nth(1, 1))
            dve.wait_ge(xe_again_loaded, a.nth(16, 16))
            nc.vector.tensor_tensor(out_sb[:], out_sb[:], xe_again[:], ALU.add).then_inc(out_done, 1)

        ROUTER = {N_STATS: norm_x, N_OUT: norm_out, N_SPLIT: split_x, R_SHIFT: shift_logits, R_PROBS: probabilities,
                  R_TOP: top, R_MATCH: match, R_PICK: pick, R_WEIGH: weigh, R_LO: weigh_lo, R_COPY: copy_weights}

        def slot(b, left=0, first=False):
            for c in range(CHUNKS):
                if c + 2 < CHUNKS:
                    if c + 2 < EC:
                        weigh_hidden(b, c + 2)
                elif left:
                    weigh_hidden(b.plus(1), c + 2 - CHUNKS)
                if left and c in ROUTER:
                    ROUTER[c](b.plus(1))
                if not first and c == Y_STATS:
                    y_stats(b.plus(-1))
                if not first and c == Y_OUT:
                    y_out(b.plus(-1))

        c = Batch(0)
        dve.wait_ge(loaded_small, 8 * 16)
        norm_x(c)
        norm_out(c)
        dve.wait_ge(set_act2, 1)
        nc.vector.tensor_tensor(sb2_sum[:], bias_cols[:, CHUNKS:CHUNKS + 1], bias_cols[:, CHUNKS + 1:CHUNKS + 2], ALU.add).then_inc(set_dve2, 1)
        nc.vector.tensor_copy(b2_hi[:], b2_sb[:]).then_inc(set_dve2, 1)
        dve.wait_ge(set_dve2, 2)
        nc.vector.tensor_tensor(b2_lo[:], b2_sb[:], b2_hi[:].bitcast(F32), ALU.subtract).then_inc(set_dve2, 1)
        split_x(c)
        shift_logits(c)
        probabilities(c)
        top(c)
        match(c)
        pick(c)
        weigh(c)
        weigh_lo(c)
        dve.wait_ge(loaded_w1, 32)
        nc.vector.tensor_copy(w1_hi[:], w1_sb[:]).then_inc(set_dve2, 1)
        dve.wait_ge(set_dve2, 4)
        nc.vector.tensor_tensor(w1_lo[:], w1_sb[:], w1_hi[:].bitcast(F32), ALU.subtract).then_inc(set_dve2, 1)
        dve.wait_ge(set_pool, 3)
        nc.vector.tensor_copy(spread[:], spread_raw[:]).then_inc(set_dve2, 1)
        copy_weights(c)
        weigh_hidden(c, 0)
        weigh_hidden(c, 1)
        slots(dve, slot)
        y_stats(Batch(NB - 1))
        y_out(Batch(NB - 1))

    @block.tensor
    def _(pe):
        mm, turn = nc.tensor.matmul, nc.tensor.transpose

        def turn_x(c):
            pe.wait_ge(norm_dve, c.nth(1, 1))
            if c.has(ROUTE, 0):
                pe.wait_ge(route_dve, c.nth(ROUTE, 0))
            for t in range(TT):
                last = turn(ps_prep[:, t * P:(t + 1) * P], xe_norm[:, t, :], ident2[:])
            last.then_inc(prep_pe2, 1)

        def make_logits(c):
            pe.wait_ge(xe_copied, c.nth(1, 1))
            for t in range(TT):
                last = mm(ps_prep[:, t * NE:(t + 1) * NE], xe_t[:, t * P:(t + 1) * P], router_sb[:], start=True, stop=True)
            last.then_inc(prep_pe2, 1)

        def turn_weights(c):
            pe.wait_ge(weight_ready, c.nth(2, 2))
            for t in range(TT):
                last = turn(ps_prep[:, t * P:(t + 1) * P], weight_split[:, t, :, :].rearrange("p a e -> p (a e)"), ident2[:])
            last.then_inc(prep_pe2, 1)

        def up(b, c):
            if c == 0:
                pe.wait_ge(split_dve, b.nth(2, 2))
                pe.wait_ge(route_dve, b.nth(ROUTE, ROUTE))
            if b.has(CHUNKS, c - 1):
                pe.wait_ge(activated, b.nth(CHUNKS, c - 1))
            if c < EC:
                last_weighted = c - 1 if c >= 2 else 0
                if b.has(EC, last_weighted):
                    pe.wait_ge(weighted, b.nth(EC, last_weighted))
                mm(ps_weight[c % 2][:], spread[:, c * P:(c + 1) * P], weight_t[b.parity][:], start=True, stop=True)
            cols = slice(c * P, (c + 1) * P)
            out = ps_hidden[c % 2][:]
            mm(out, w1_hi[:, cols], xe_hi[b.parity][:], start=True, stop=False)
            mm(out, w1_hi[:, cols], xe_lo[b.parity][:], start=False, stop=False)
            mm(out, w1_lo[:, cols], xe_hi[b.parity][:], start=False, stop=True).then_inc(up_done, 1)

        def down(b, c):
            out = ps_y[b.parity][:]
            if c == 0:
                if b.has(1, -1):
                    pe.wait_ge(ye_copied, b.nth(1, -1))
                mm(out, b2_hi[:], weight_t[b.parity][:], start=True, stop=False)
                mm(out, b2_lo[:], weight_t[b.parity][:], start=False, stop=False)
            if c < EC:
                pe.wait_ge(weighted, b.nth(EC, c + 1))
            else:
                pe.wait_ge(activated, b.nth(CHUNKS, c + 1))
            mm(out, w2_sb[:, c, :], gated[:, c % 4, :], start=False, stop=(c == CHUNKS - 1)).then_inc(down_done, 1)

        def turn_y(a):
            pe.wait_ge(ye_copied, a.nth(1, 1))
            if a.has(1, 0):
                pe.wait_ge(post_dve2, a.nth(1, 0))
            for t in range(TT):
                last = turn(ps_post[:, t * P:(t + 1) * P], ye_t[:, t * P:(t + 1) * P], ident2[:])
            last.then_inc(post_pe2, 1)

        def slot(b, left=0, first=False):
            for c in range(CHUNKS):
                down(b, c)
                if c + 2 < CHUNKS:
                    up(b, c + 2)
                elif left:
                    up(b.plus(1), c + 2 - CHUNKS)
                if left and c == N_TURN:
                    turn_x(b.plus(1))
                if left and c == R_LOGITS:
                    make_logits(b.plus(1))
                if left and c == R_TURN:
                    turn_weights(b.plus(1))
                if not first and c == Y_TURN:
                    turn_y(b.plus(-1))

        pe.wait_ge(loaded_small, 8 * 16)
        turn(ps_post[:, 0:CHUNKS + ES], bias_rows[:], ident2[0:CHUNKS + ES, 0:CHUNKS + ES]).then_inc(set_pe2, 1)
        c = Batch(0)
        turn_x(c)
        make_logits(c)
        turn_weights(c)
        pe.wait_ge(set_dve2, 6)
        pe.wait_ge(loaded_w2, 32)
        up(c, 0)
        up(c, 1)
        slots(pe, slot)
        turn_y(Batch(NB - 1))


def layer_kernel(nc, x, Wq, Wk, Wv, Wo, qA, qB, kA, kB, vA, vB, oA, oB, router_w, router_b,
                 w1, b1, w2, b2, sw1, sb1, sw2, sb2, cos_t, sin_t, ident_d, sel_d, out):
    x1_dram = nc.dram_tensor("x_after_attention", x.shape, F32, kind="Internal").ap()
    with ExitStack() as ctx:
        attention_block(nc, ctx, (x, Wq, Wk, Wv, Wo, qA, qB, kA, kB, vA, vB, oA, oB, cos_t, sin_t, ident_d, sel_d), x1_dram)
    with ExitStack() as ctx:
        experts_block(nc, ctx, (router_w, router_b, w1, b1, w2, b2, sw1, sb1, sw2, sb2, ident_d), x1_dram, out)


_INS = ['L0_attn_x', 'L0_attn_Wq', 'L0_attn_Wk', 'L0_attn_Wv', 'L0_attn_Wo', 'L0_attn_qA', 'L0_attn_qB', 'L0_attn_kA',
        'L0_attn_kB', 'L0_attn_vA', 'L0_attn_vB', 'L0_attn_oA', 'L0_attn_oB', 'L0_ffn_router_w', 'L0_ffn_router_b',
        'L0_ffn_w1', 'L0_ffn_b1', 'L0_ffn_w2', 'L0_ffn_b2', 'L0_ffn_sw1', 'L0_ffn_sb1', 'L0_ffn_sw2', 'L0_ffn_sb2']


def _constants(seq):
    import numpy as np
    inv_freq = (1.0 / np.float32(10000.0) ** (np.arange(0, HD, 2, dtype=np.float32) / np.float32(HD))).astype(np.float32)
    freqs = np.arange(seq, dtype=np.float32)[:, None] * inv_freq[None, :]
    def tiled(a):
        return np.ascontiguousarray(a.astype(np.float32).reshape(seq // P, P, HALF).transpose(1, 0, 2))
    pair_head = np.arange(NQ * HD) // HD
    sel = np.zeros((32 + NQ, NQ * HD), np.float32)
    sel[0:NQ] = sel[32:32 + NQ] = np.arange(NQ)[:, None] == pair_head[None, :]
    return {'cos': tiled(np.cos(freqs)), 'sin': tiled(np.sin(freqs)), 'ident': np.eye(P, dtype=np.float32), 'sel': sel}


def kernel(**inputs):
    import numpy as _np
    import concourse.bacc as _bacc
    from concourse import mybir as _mybir
    from concourse.bass_utils import run_bass_kernel_spmd as _run

    nc = _bacc.Bacc("TRN2", target_bir_lowering=False, num_devices=1)
    arrays = {f"in_{name}_dram": _np.ascontiguousarray(inputs[name]) for name in _INS}
    shape = inputs['L0_attn_x'].shape
    arrays.update({f"const_{name}_dram": a for name, a in _constants(shape[1]).items()})
    args = [nc.dram_tensor(name, a.shape, _mybir.dt.from_np(a.dtype), kind="ExternalInput").ap()
            for name, a in arrays.items()]
    args.append(nc.dram_tensor("out_0_dram", shape, _mybir.dt.float32, kind="ExternalOutput").ap())
    layer_kernel(nc, *args)
    r = _run(nc, [arrays], core_ids=[0])
    return r.results[0]["out_0_dram"]
```

```python
from contextlib import ExitStack

import concourse.bass as bass
from concourse import mybir

F32 = mybir.dt.float32
F32R = mybir.dt.float32r
ALU = mybir.AluOpType
ACT = mybir.ActivationFunctionType
AX_X = mybir.AxisListType.X

P = 128
NQ, NKV, HD, RANK = 16, 4, 64, 8
HALF = HD // 2
NE, EH, TOPK = 64, 32, 8
ES, HS = 2, 256
EPS = 1e-5
LORA_SCALE = 16 / RANK
QK_SCALE = HD ** -0.5


class Batch:

    def __init__(self, const, reg=None):
        self.const, self.reg = const, reg
        self.parity = const % 2

    def plus(self, n):
        return Batch(self.const + n, self.reg)

    def index(self):
        return self.const if self.reg is None else self.reg * 2 + self.const

    def nth(self, per_batch, k):
        base = self.const * per_batch + k
        return base if self.reg is None else self.reg * (2 * per_batch) + base

    def has(self, per_batch, k):
        return self.const * per_batch + k > 0


def attention_block(nc, ctx, args, x1_dram):
    x, Wq, Wk, Wv, Wo, qA, qB, kA, kB, vA, vB, oA, oB, cos_t, sin_t, ident_d, sel_d = args
    NB, S, D = x.shape
    TT = S // P
    UNITS = NQ * TT
    GROUPS = UNITS // 4
    PAIRS = NQ // 2
    QKV = (NQ + 2 * NKV) * HD
    OCH = QKV // P
    PROJ = TT * (QKV // 512)
    assert D == P and S == 512 and NB % 2 == 0 and NB >= 4

    def sb(name, shape, dt=F32):
        return ctx.enter_context(nc.sbuf_tensor(name, shape, dt))

    def psum(name):
        return ctx.enter_context(nc.psum_tensor(name, [P, 512], F32))

    def sem(name):
        return ctx.enter_context(nc.semaphore(name))

    q_stack = [sb(f"q_stack{i}", [P, NQ, S], F32R) for i in range(2)]
    k_stack = [sb(f"k_stack{i}", [P, NKV, 2, S], F32R) for i in range(2)]
    v_sb = [sb(f"v_sb{i}", [P, TT, NKV * HD]) for i in range(2)]
    probs = sb("probs", [P, 4, S])
    probs_t = [sb(f"probs_t{i}", [P, 2, 4, 2 * P]) for i in range(2)]
    o_t = sb("o_t", [P, PAIRS, S])
    wqkv_hi = sb("wqkv_hi", [P, QKV], F32R)
    wqkv_lo = sb("wqkv_lo", [P, QKV], F32R)
    wo_hi = sb("wo_hi", [P, PAIRS, D], F32R)
    wo_lo = sb("wo_lo", [P, PAIRS, D], F32R)
    o_hi = sb("o_hi", [P, 3, S], F32R)
    o_lo = sb("o_lo", [P, 2, S], F32R)
    x_in = sb("x_in", [P, TT, D])
    x_norm = sb("x_norm", [P, TT, D])
    xt_hi = sb("xt_hi", [P, S], F32R)
    xt_lo = sb("xt_lo", [P, S], F32R)
    rope_c = [sb(f"rope_c{i}", [P, 512]) for i in range(2)]
    rope_s = [sb(f"rope_s{i}", [P, 512]) for i in range(2)]
    cos_sb = sb("cos_sb", [P, TT, HALF])
    sin_sb = sb("sin_sb", [P, TT, HALF])
    ident = sb("ident", [P, P])
    INV_ROWS = 32 + NQ
    sel = sb("sel", [INV_ROWS, PAIRS * P], F32R)
    sums = [sb(f"sums{i}", [P, TT, NQ]) for i in range(2)]
    neg_max = sb("neg_max", [P, 4])
    inv_sum = sb("inv_sum", [P, TT, NQ])
    inv_split = sb("inv_split", [INV_ROWS, S], F32R)
    y_t = sb("y_t", [P, S])
    x_again = sb("x_again", [P, TT, D])
    x1 = sb("x1", [P, TT, D])
    stats = sb("stats", [P, 2, TT, 6])
    mean_var = sb("mean_var", [P, 2, TT, 2])
    rstd = sb("rstd", [P, 2, TT])
    minus_half = sb("minus_half", [P, TT])
    eps = sb("eps", [P, TT])

    raw = probs_t[0][:, :, :, :].rearrange("p a b c -> p (a b c)")
    raw2 = probs_t[1][:, :, :, :].rearrange("p a b c -> p (a b c)")
    w_raw = raw[:, 0:OCH * P].rearrange("p (o d) -> p o d", o=OCH)
    b_raw = raw[:, OCH * P:OCH * P + (OCH + 1) * RANK].rearrange("p (o r) -> p o r", o=OCH + 1)
    wo_raw = raw2[:, 0:PAIRS * P]
    sel_raw = raw2[0:INV_ROWS, PAIRS * P:2 * PAIRS * P]
    lora_b = o_t[0:RANK, :, :].rearrange("p a b -> p (a b)")[:, 0:(OCH + 1) * P].rearrange("p (o d) -> p o d", o=OCH + 1)
    lora_a = o_t[0:RANK, :, :].rearrange("p a b -> p (a b)")[:, 1792:1792 + 3 * P].rearrange("p (o d) -> p o d", o=3)
    oa_raw = o_t[0:RANK, :, :].rearrange("p a b -> p (a b)")[:, 2304:2304 + 1024]
    w_fold = probs[:, :, :]
    wo_fold = o_t[:, 0:2, :]

    ps_scores = [psum(f"ps_scores{i}") for i in range(3)]
    ps_turned = [psum(f"ps_turned{i}") for i in range(2)]
    ps_out = psum("ps_out")
    ps_prep = psum("ps_prep")
    ps_post = psum("ps_post")

    ident_loaded = sem("ident_loaded")
    const_loaded = sem("const_loaded")
    b_loaded = sem("b_loaded")
    w_loaded = sem("w_loaded")
    wo_loaded = sem("wo_loaded")
    set_pe = sem("set_pe")
    set_act = sem("set_act")
    set_dve = sem("set_dve")
    ready_pool = sem("ready_pool")
    scored = sem("scored")
    maxed = sem("maxed")
    exped = sem("exped")
    turned = sem("turned")
    turned_out = sem("turned_out")
    attended = sem("attended")
    o_copied = sem("o_copied")
    x_loaded = sem("x_loaded")
    prep_pe = sem("prep_pe")
    prep_free = sem("prep_free")
    prep_dve = sem("prep_dve")
    prep_stat = sem("prep_stat")
    prep_rstd = sem("prep_rstd")
    pool_chain = sem("pool_chain")
    xt_hi_done = sem("xt_hi_done")
    roped = sem("roped")
    rope_sum = sem("rope_sum")
    stacked_hi = sem("stacked_hi")
    stacked = sem("stacked")
    post_pe = sem("post_pe")
    inv_done = sem("inv_done")
    inv_hi_done = sem("inv_hi_done")
    inv_lo_done = sem("inv_lo_done")
    scaled = sem("scaled")
    o_high = sem("o_high")
    o_low = sem("o_low")
    projected = sem("projected")
    y_copied = sem("y_copied")
    post_stat = sem("post_stat")
    post_rstd = sem("post_rstd")
    x_again_loaded = sem("x_again_loaded")
    post_dve = sem("post_dve")
    x1_done = sem("x1_done")
    x1_stored = sem("x1_stored")

    def unit(u):
        g = u // 4
        pair, half = g // 2, g % 2
        qt = 2 * half + u % 4 // 2
        return pair * 2 + u % 2, qt

    assert UNITS % 3 == 1

    def bank_of(u):
        return ps_prep if u == UNITS - 1 else ps_scores[u % 3]

    def before_in_bank(u):
        return u - 4 if u < 3 else u - 3

    def tile_and_columns(n):
        return n // 3, (2, 0, 1)[n % 3]

    jobs = [("proj", 0)]
    for n in range(PROJ):
        if n + 1 < PROJ:
            jobs.append(("proj", n + 1))
        jobs.append(("turn", n))
    job_at = {10 + 2 * j: (j, job) for j, job in enumerate(jobs)}
    JOBS = len(jobs)
    job_of = {job: j for j, job in enumerate(jobs)}
    assert max(job_at) < UNITS - 4
    PREP_PE = 1 + JOBS

    ATTEND_AT = {1: (0,), 2: (1,), 3: (2, 3)}

    PREP_STATS, PREP_NORM, PREP_X = 1, 5, 7

    POST_INV, POST_SCALE = 2, 3
    POST_PROJ = POST_SCALE + PAIRS
    POST_Y = POST_PROJ + PAIRS
    POST_NORM = [POST_Y + 6 + 2 * t for t in range(TT)]
    POST_SUM = POST_NORM[-1] + 2
    PER_POST_PE = 1 + PAIRS + 1

    def prep_bank(c, job):
        if c.reg is None and c.const == 0:
            return ps_scores[job[1] % 3] if job[0] == "proj" else ps_turned[job[1] % 2]
        return ps_prep

    def spread_bank(pair, alone):
        return ps_scores[pair % 3] if alone else ps_post

    def lora_of(o):
        return 0 if o < 8 else 1 if o < 10 else 2

    x_tiles = x.rearrange("b (t p) d -> p (b t) d", p=P)
    x1_tiles = x1_dram.rearrange("b (t p) d -> p (b t) d", p=P)
    block = ctx.enter_context(nc.Block())

    def slots(eng, slot):
        slot(Batch(0), first=True, left=NB - 1)
        slot(Batch(1), left=NB - 2)
        if NB > 4:
            with eng.Fori(0, NB // 2 - 2) as i:
                slot(Batch(2, i), left=2)
                slot(Batch(3, i), left=2)
        slot(Batch(NB - 2), left=1)
        slot(Batch(NB - 1), left=0)

    @block.sync
    def _(sp):
        sp.dma_start(ident[:], ident_d).then_inc(ident_loaded, 16)
        sp.dma_start(x_in[:], x_tiles[:, 0:TT, :]).then_inc(x_loaded, 16)
        sp.dma_start(b_raw[:, 0:8, :], qB.rearrange("(o p) r -> p o r", p=P)).then_inc(b_loaded, 16)
        sp.dma_start(b_raw[:, 8:10, :], kB.rearrange("(o p) r -> p o r", p=P)).then_inc(b_loaded, 16)
        sp.dma_start(b_raw[:, 10:12, :], vB.rearrange("(o p) r -> p o r", p=P)).then_inc(b_loaded, 16)
        sp.dma_start(b_raw[:, 12, :], oB).then_inc(b_loaded, 16)
        sp.dma_start(cos_sb[:], cos_t).then_inc(const_loaded, 16)
        sp.dma_start(sin_sb[:], sin_t).then_inc(const_loaded, 16)
        sp.dma_start(sel_raw, sel_d).then_inc(const_loaded, 16)

        def load_x(c):
            sp.wait_ge(prep_dve, c.nth(1, 0))
            sp.dma_start(x_in[:], x_tiles[:, bass.ds(c.index() * TT, TT), :]).then_inc(x_loaded, 16)

        def store_x1(a):
            sp.wait_ge(x1_done, a.nth(1, 1))
            sp.dma_start(x1_tiles[:, bass.ds(a.index() * TT, TT), :], x1[:]).then_inc(x1_stored, 16)

        def load_x_again(a):
            if a.has(1, 0):
                sp.wait_ge(x1_done, a.nth(1, 0))
            sp.dma_start(x_again[:], x_tiles[:, bass.ds(a.index() * TT, TT), :]).then_inc(x_again_loaded, 16)

        def slot(b, left=0, first=False):
            if left >= 2:
                load_x(b.plus(2))
            if not first:
                load_x_again(b.plus(-1))
                store_x1(b.plus(-1))

        load_x(Batch(1))
        slots(sp, slot)
        load_x_again(Batch(NB - 1))
        store_x1(Batch(NB - 1))
        sp.wait_ge(x1_stored, 16 * NB)


    @block.gpsimd
    def _(pool):
        nc.gpsimd.memset(minus_half[:], -0.5)
        nc.gpsimd.memset(eps[:], EPS).then_inc(ready_pool, 1)
        pool.wait_ge(ready_pool, 1)

        def rstd_of(which, b, stat, done, chain_value):
            pool.wait_ge(stat, b.nth(1, 1))
            nc.gpsimd.tensor_tensor(rstd[:, which, :], mean_var[:, which, :, 1], eps[:], ALU.add).then_inc(pool_chain, 1)
            pool.wait_ge(pool_chain, chain_value)
            nc.gpsimd.tensor_tensor(rstd[:, which, :], rstd[:, which, :], minus_half[:], ALU.pow).then_inc(done, 1)

        def rotate(c, n):
            heads = 8 if tile_and_columns(n)[1] < 2 else NKV
            c4 = rope_c[n % 2][:, 0:heads * HD].rearrange("p (h e i) -> p h e i", e=2, i=HALF)
            s4 = rope_s[n % 2][:, 0:heads * HD].rearrange("p (h e i) -> p h e i", e=2, i=HALF)
            pool.wait_ge(roped, c.nth(PROJ, n + 1))
            nc.gpsimd.tensor_tensor(c4[:, :, 0, :], c4[:, :, 0, :], s4[:, :, 1, :], ALU.subtract)
            nc.gpsimd.tensor_tensor(c4[:, :, 1, :], c4[:, :, 1, :], s4[:, :, 0, :], ALU.add).then_inc(rope_sum, 1)

        def out_low(a, pair):
            pool.wait_ge(o_high, a.nth(PAIRS, pair + 1))
            if a.has(PAIRS, pair - 1):
                pool.wait_ge(projected, a.nth(PAIRS, pair - 1))
            nc.gpsimd.tensor_tensor(o_lo[:, pair % 2, :], o_t[:, pair, :], o_hi[:, pair % 3, :].bitcast(F32),
                                    ALU.subtract).then_inc(o_low, 1)

        def slot(b, left=0, first=False):
            for u in range(UNITS):
                if left and u == PREP_STATS:
                    rstd_of(0, b.plus(1), prep_stat, prep_rstd, 2 if first else b.nth(2, 1))
                if not first and POST_PROJ - 2 <= u < POST_PROJ - 2 + PAIRS:
                    out_low(b.plus(-1), u - POST_PROJ + 2)
                if not first and u == POST_Y + 2:
                    rstd_of(1, b.plus(-1), post_stat, post_rstd, b.nth(2, 2 if left else 1))
                if left and u in job_at and job_at[u][1][0] == "proj":
                    rotate(b.plus(1), job_at[u][1][1])

        rstd_of(0, Batch(0), prep_stat, prep_rstd, 1)
        for n in range(PROJ):
            rotate(Batch(0), n)
        slots(pool, slot)
        for pair in range(PAIRS):
            out_low(Batch(NB - 1), pair)
        rstd_of(1, Batch(NB - 1), post_stat, post_rstd, 2 * NB)

    @block.scalar
    def _(act):
        def x_hi(c):
            act.wait_ge(prep_pe, c.nth(PREP_PE, 1))
            nc.scalar.activation(xt_hi[:], ps_prep[:], ACT.Copy).then_inc(xt_hi_done, 1)

        def stack_hi(c, j, n):
            tt, col = tile_and_columns(n)
            cols = slice(tt * P, tt * P + P)
            act.wait_ge(prep_pe, c.nth(PREP_PE, 1 + j + 1))
            bank = prep_bank(c, ("turn", n))
            for s in range(2):
                rows = slice(s * HD, s * HD + HD)
                if col < 2:
                    src = bank[rows, :].rearrange("p (h t) -> p h t", h=4)
                    last = nc.scalar.activation(q_stack[c.parity][0:HD, 8 * col + s:8 * col + 8:2, cols], src, ACT.Copy)
                else:
                    src = bank[rows, 0:2 * P].rearrange("p (h t) -> p h t", h=2)
                    for d in range(2):
                        last = nc.scalar.activation(k_stack[c.parity][d * HD:d * HD + HD, s:NKV:2, 0, cols], src, ACT.Copy)
                last.then_inc(stacked_hi, 1)

        def exp(b, u):
            head, qt = unit(u)
            act.wait_ge(maxed, b.nth(UNITS, u + 1))
            if b.has(UNITS, u - 3):
                act.wait_ge(turned, b.nth(UNITS, u - 3))
            nc.scalar.activation(probs[:, u % 4, :], bank_of(u)[:], ACT.Exp,
                                 bias=neg_max[:, u % 4:u % 4 + 1],
                                 accum_out=sums[b.parity][:, qt, head:head + 1]).then_inc(exped, 1)

        def copy_turned(b, u):
            g = u // 4
            act.wait_ge(turned, b.nth(UNITS, u + 1))
            if u % 4 == 0 and b.has(GROUPS, g - 1):
                act.wait_ge(attended, b.nth(GROUPS, g - 1))
            qo = u % 4 // 2 * P
            nc.scalar.activation(probs_t[g % 2][:, u % 2, :, qo:qo + P],
                                 ps_turned[u % 2][:].rearrange("p (k q) -> p k q", k=4), ACT.Copy).then_inc(turned_out, 1)

        def copy_out(b, pair):
            act.wait_ge(attended, b.nth(GROUPS, 2 * pair + 2))
            if b.has(PAIRS, pair + 1 - PAIRS):
                act.wait_ge(projected, b.nth(PAIRS, pair + 1 - PAIRS))
            nc.scalar.activation(o_t[:, pair, :], ps_out[:], ACT.Copy).then_inc(o_copied, 1)

        def inverse_hi(a):
            act.wait_ge(post_pe, a.nth(PER_POST_PE, 1))
            nc.scalar.activation(inv_split[0:NQ, :], ps_post[0:NQ, :], ACT.Copy).then_inc(inv_hi_done, 1)

        def copy_y(a):
            act.wait_ge(projected, a.nth(PAIRS, PAIRS))
            nc.scalar.activation(y_t[:], ps_post[:], ACT.Copy).then_inc(y_copied, 1)

        def slot(b, left=0, first=False):
            for u in range(UNITS):
                if u % 8 == 4 and (u >= 12 or not first):
                    copy_out(b if u >= 12 else b.plus(-1), (u // 8 - 1) % PAIRS)
                if u + 2 < UNITS:
                    exp(b, u + 2)
                elif left:
                    exp(b.plus(1), u + 2 - UNITS)
                copy_turned(b, u)
                if not first and u == POST_INV:
                    inverse_hi(b.plus(-1))
                if not first and u == POST_Y:
                    copy_y(b.plus(-1))
                if left and u == PREP_X:
                    x_hi(b.plus(1))
                if left and u in job_at:
                    j, job = job_at[u]
                    if job[0] == "turn":
                        stack_hi(b.plus(1), j, job[1])

        for n, a in enumerate((qA, kA, vA)):
            act.dma_start(lora_a[:, n, :], a).then_inc(w_loaded, 16)
        act.dma_start(oa_raw, oA).then_inc(w_loaded, 16)
        act.dma_start(w_raw[:, 0:8, :], Wq.rearrange("(o p) d -> p o d", p=P)).then_inc(w_loaded, 16)
        act.dma_start(w_raw[:, 8:10, :], Wk.rearrange("(o p) d -> p o d", p=P)).then_inc(w_loaded, 16)
        act.dma_start(w_raw[:, 10:12, :], Wv.rearrange("(o p) d -> p o d", p=P)).then_inc(w_loaded, 16)
        act.dma_start(wo_raw, Wo).then_inc(wo_loaded, 16)
        x_hi(Batch(0))
        act.wait_ge(set_pe, 1)
        nc.scalar.activation(lora_b[:, 0:4, :], ps_scores[0][0:RANK, :], ACT.Copy, scale=LORA_SCALE)
        nc.scalar.activation(lora_b[:, 4:8, :], ps_scores[1][0:RANK, :], ACT.Copy, scale=LORA_SCALE)
        nc.scalar.activation(lora_b[:, 8:12, :], ps_scores[2][0:RANK, :], ACT.Copy, scale=LORA_SCALE)
        nc.scalar.activation(lora_b[:, 12, :], ps_turned[0][0:RANK, 0:P], ACT.Copy, scale=LORA_SCALE).then_inc(set_act, 1)
        for n in range(3):
            act.wait_ge(set_pe, 2 + n)
            for c0, c1, is_v in ((0, 512, False),) if n < 2 else ((0, 256, False), (256, 512, True)):
                src, dst = ps_scores[n][:, c0:c1], w_fold[:, n, c0:c1]
                if not is_v:
                    src = src.rearrange("p (h i e) -> p h e i", e=2, i=HALF)
                    dst = dst.rearrange("p (h e i) -> p h e i", e=2, i=HALF)
                last = nc.scalar.activation(dst, src, ACT.Copy, scale=QK_SCALE if n < 2 else 1.0)
            last.then_inc(set_act, 1)
        for n in range(PROJ):
            if n == 1:
                act.wait_ge(set_pe, 5)
                nc.scalar.activation(wo_fold[:, 0, :], ps_out[:], ACT.Copy)
                nc.scalar.activation(wo_fold[:, 1, :], ps_post[:], ACT.Copy).then_inc(set_act, 1)
            stack_hi(Batch(0), job_of["turn", n], n)
        exp(Batch(0), 0)
        exp(Batch(0), 1)
        slots(act, slot)
        copy_out(Batch(NB - 1), PAIRS - 1)
        inverse_hi(Batch(NB - 1))
        copy_y(Batch(NB - 1))

    @block.vector
    def _(dve):
        def variance(which, src, stat):
            for t in range(TT):
                nc.vector.bn_stats(stats[:, which, t, :], src[:, t, :])
            dve.drain()
            for t in range(TT):
                last = nc.vector.bn_aggr(mean_var[:, which, t, :], stats[:, which, t, :])
            last.then_inc(stat, 1)

        def normalise(which, out, src, t):
            return nc.vector.tensor_scalar(out[:, t, :], src[:, t, :], mean_var[:, which, t, 0:1], rstd[:, which, t:t + 1],
                                           ALU.subtract, ALU.mult)

        def norm_x(c):
            dve.wait_ge(x_loaded, c.nth(16, 16))
            variance(0, x_in, prep_stat)

        def norm_x_out(c):
            dve.wait_ge(prep_rstd, c.nth(1, 1))
            if c.has(PREP_PE, 1 - PREP_PE):
                dve.wait_ge(prep_pe, c.nth(PREP_PE, 1 - PREP_PE))
            for t in range(TT):
                last = normalise(0, x_norm, x_in, t)
            last.then_inc(prep_dve, 1)

        def x_lo(c):
            dve.wait_ge(xt_hi_done, c.nth(1, 1))
            nc.vector.tensor_tensor(xt_lo[:], ps_prep[:], xt_hi[:].bitcast(F32), ALU.subtract).then_inc(prep_free, 1)

        def rope_products(c, j, n):
            (tt, col), r = tile_and_columns(n), n % 2
            dve.wait_ge(prep_pe, c.nth(PREP_PE, 1 + j + 1))
            width = 512 if col < 2 else NKV * HD
            bank = prep_bank(c, ("proj", n))
            src = bank[:, 0:width].rearrange("p (h i) -> p h i", i=HALF)
            cs = cos_sb[:, tt, :].unsqueeze(1).to_broadcast([P, width // HALF, HALF])
            sn = sin_sb[:, tt, :].unsqueeze(1).to_broadcast([P, width // HALF, HALF])
            nc.vector.tensor_tensor(rope_c[r][:, 0:width].rearrange("p (h i) -> p h i", i=HALF), src, cs, ALU.mult)
            if col == 2:
                if c.has(GROUPS, -GROUPS):
                    dve.wait_ge(attended, c.nth(GROUPS, -GROUPS))
                nc.vector.tensor_copy(v_sb[c.parity][:, tt, :], bank[:, width:512])
            nc.vector.tensor_tensor(rope_s[r][:, 0:width].rearrange("p (h i) -> p h i", i=HALF), src, sn,
                                    ALU.mult).then_inc(roped, 1)

        def stack_lo(c, n):
            tt, col = tile_and_columns(n)
            cols = slice(tt * P, tt * P + P)
            bank = prep_bank(c, ("turn", n))
            for s in range(2):
                dve.wait_ge(stacked_hi, c.nth(2 * PROJ, 2 * n + s + 1))
                rows = slice(s * HD, s * HD + HD)
                if col < 2:
                    heads = q_stack[c.parity][:, 8 * col + s:8 * col + 8:2, cols]
                    src = bank[rows, :].rearrange("p (h t) -> p h t", h=4)
                    last = nc.vector.tensor_tensor(heads[HD:2 * HD], src, heads[0:HD].bitcast(F32), ALU.subtract)
                else:
                    src = bank[rows, 0:2 * P].rearrange("p (h t) -> p h t", h=2)
                    for d in range(2):
                        heads = k_stack[c.parity][d * HD:d * HD + HD, s:NKV:2, :, cols]
                        last = nc.vector.tensor_tensor(heads[:, :, 1, :], src, heads[:, :, 0, :].bitcast(F32), ALU.subtract)
            last.then_inc(stacked, 1)

        def do_job(c, j, job):
            if job[0] == "proj":
                rope_products(c, j, job[1])
            else:
                stack_lo(c, job[1])

        def maxima(b, u):
            dve.wait_ge(scored, b.nth(UNITS, u + 1))
            if b.has(UNITS, u - 3):
                dve.wait_ge(exped, b.nth(UNITS, u - 3))
            nc.vector.reduce_max(neg_max[:, u % 4:u % 4 + 1], bank_of(u)[:], AX_X, negate=True).then_inc(maxed, 1)

        def inverse(a):
            dve.wait_ge(exped, a.nth(UNITS, UNITS))
            if a.has(PER_POST_PE, 1 - PER_POST_PE):
                dve.wait_ge(post_pe, a.nth(PER_POST_PE, 1 - PER_POST_PE))
            nc.vector.reciprocal(inv_sum[:], sums[a.parity][:]).then_inc(inv_done, 1)

        def inverse_lo(a):
            dve.wait_ge(inv_hi_done, a.nth(1, 1))
            nc.vector.tensor_tensor(inv_split[32:32 + NQ, :], ps_post[0:NQ, :], inv_split[0:NQ, :].bitcast(F32), ALU.subtract).then_inc(inv_lo_done, 1)

        def scale_out(a, pair, alone=False):
            dve.wait_ge(post_pe, a.nth(PER_POST_PE, 2 + pair))
            dve.wait_ge(o_copied, a.nth(PAIRS, pair + 1))
            nc.vector.tensor_tensor(o_t[:, pair, :], o_t[:, pair, :], spread_bank(pair, alone)[:], ALU.mult).then_inc(scaled, 1)

        def out_hi(a, pair):
            dve.wait_ge(scaled, a.nth(PAIRS, pair + 1))
            if a.has(PAIRS, pair - 2):
                dve.wait_ge(projected, a.nth(PAIRS, pair - 2))
            nc.vector.tensor_copy(o_hi[:, pair % 3, :], o_t[:, pair, :]).then_inc(o_high, 1)

        def y_stats(a):
            dve.wait_ge(post_pe, a.nth(PER_POST_PE, PER_POST_PE))
            variance(1, ps_post[:].rearrange("p (t d) -> p t d", t=TT), post_stat)

        def y_norm(a, t):
            if t == 0:
                dve.wait_ge(post_rstd, a.nth(1, 1))
                if a.has(16, 0):
                    dve.wait_ge(x1_stored, a.nth(16, 0))
            normalise(1, x1, ps_post[:].rearrange("p (t d) -> p t d", t=TT), t).then_inc(post_dve, 1)

        def residual(a):
            dve.wait_ge(post_dve, a.nth(TT, TT))
            dve.wait_ge(x_again_loaded, a.nth(16, 16))
            nc.vector.tensor_tensor(x1[:], x1[:], x_again[:], ALU.add).then_inc(x1_done, 1)

        def slot(b, left=0, first=False):
            for u in range(UNITS):
                if u + 3 < UNITS:
                    maxima(b, u + 3)
                elif left:
                    maxima(b.plus(1), u + 3 - UNITS)
                if left and u == PREP_STATS:
                    norm_x(b.plus(1))
                if left and u == PREP_NORM:
                    norm_x_out(b.plus(1))
                if left and u == PREP_X:
                    x_lo(b.plus(1))
                if left and u in job_at:
                    do_job(b.plus(1), *job_at[u])
                if not first:
                    a = b.plus(-1)
                    if u == 0:
                        inverse(a)
                    if u == POST_INV:
                        inverse_lo(a)
                    if POST_SCALE <= u < POST_SCALE + PAIRS:
                        scale_out(a, u - POST_SCALE)
                    if POST_PROJ - 2 <= u < POST_PROJ - 2 + PAIRS:
                        out_hi(a, u - POST_PROJ + 2)
                    if u == POST_Y + 2:
                        y_stats(a)
                    if u in POST_NORM:
                        y_norm(a, POST_NORM.index(u))
                    if u == POST_SUM:
                        residual(a)

        c = Batch(0)
        norm_x(c)
        nc.vector.memset(inv_split[:].bitcast(F32), 0.0)
        norm_x_out(c)
        x_lo(c)
        dve.wait_ge(const_loaded, 48)
        nc.vector.tensor_copy(sel[:], sel_raw).then_inc(set_dve, 1)
        for n in range(3):
            cols = slice(512 * n, 512 * n + 512)
            dve.wait_ge(set_act, 2 + n)
            nc.vector.tensor_copy(wqkv_hi[:, cols], w_fold[:, n, :]).then_inc(set_dve, 1)
            dve.wait_ge(set_dve, 2 + 2 * n)
            nc.vector.tensor_tensor(wqkv_lo[:, cols], w_fold[:, n, :], wqkv_hi[:, cols].bitcast(F32), ALU.subtract).then_inc(set_dve, 1)
        for n in range(PROJ + 2):
            if n < PROJ:
                rope_products(c, job_of["proj", n], n)
            if n >= 2:
                stack_lo(c, n - 2)
        dve.wait_ge(set_act, 5)
        nc.vector.tensor_copy(wo_hi[:].rearrange("p (a c) d -> p a (c d)", a=2), wo_fold).then_inc(set_dve, 1)
        dve.wait_ge(set_dve, 8)
        nc.vector.tensor_tensor(wo_lo[:].rearrange("p (a c) d -> p a (c d)", a=2), wo_fold,
                                wo_hi[:].rearrange("p (a c) d -> p a (c d)", a=2).bitcast(F32), ALU.subtract).then_inc(set_dve, 1)
        for u in range(3):
            maxima(c, u)
        slots(dve, slot)
        a = Batch(NB - 1)
        inverse(a)
        inverse_lo(a)
        for pair in range(PAIRS):
            scale_out(a, pair, alone=True)
            out_hi(a, pair)
        y_stats(a)
        for t in range(TT):
            y_norm(a, t)
        residual(a)

    @block.tensor
    def _(pe):
        mm, turn = nc.tensor.matmul, nc.tensor.transpose
        def turn_x(c):
            pe.wait_ge(prep_dve, c.nth(1, 1))
            if c.has(UNITS, -UNITS):
                pe.wait_ge(exped, c.nth(UNITS, -UNITS))
            elif c.has(PREP_PE, 0):
                pe.wait_ge(stacked, c.nth(PROJ, 0))
            for t in range(TT):
                last = turn(ps_prep[:, t * P:(t + 1) * P], x_norm[:, t, :], ident[:])
            last.then_inc(prep_pe, 1)

        def wait_prep_free(c, j):
            kind, n = jobs[j]
            if prep_bank(c, jobs[j]) is not ps_prep:
                if kind == "proj" and n >= 3:
                    pe.wait_ge(roped, n - 2)
                if kind == "turn" and n >= 2:
                    pe.wait_ge(stacked, n - 1)
            elif j == 0:
                pe.wait_ge(prep_free, c.nth(1, 1))
            elif jobs[j - 1][0] == "proj":
                pe.wait_ge(roped, c.nth(PROJ, jobs[j - 1][1] + 1))
            else:
                pe.wait_ge(stacked, c.nth(PROJ, jobs[j - 1][1] + 1))

        def do_job(c, j, job):
            wait_prep_free(c, j)
            n, bank = job[1], prep_bank(c, job)
            tt, col = tile_and_columns(n)
            if job[0] == "proj":
                rows, cols = slice(tt * P, tt * P + P), slice(col * 512, col * 512 + 512)
                mm(bank[:], xt_hi[:, rows], wqkv_hi[:, cols], start=True, stop=False)
                mm(bank[:], xt_hi[:, rows], wqkv_lo[:, cols], start=False, stop=False)
                mm(bank[:], xt_lo[:, rows], wqkv_hi[:, cols], start=False, stop=True).then_inc(prep_pe, 1)
            else:
                pe.wait_ge(rope_sum, c.nth(PROJ, n + 1))
                for h in range(4 if col < 2 else 2):
                    last = turn(bank[:, h * P:(h + 1) * P], rope_c[n % 2][:, h * P:(h + 1) * P], ident[:])
                last.then_inc(prep_pe, 1)

        def scores(b, u, left=1):
            head, qt = unit(u)
            if u == 0:
                pe.wait_ge(stacked, b.nth(PROJ, PROJ))
            before = before_in_bank(u) + 1
            if u == UNITS - 1:
                if left:
                    pe.wait_ge(stacked, b.nth(PROJ, 2 * PROJ))
            elif b.has(UNITS, before):
                pe.wait_ge(exped, b.nth(UNITS, before))
            out = bank_of(u)
            q = q_stack[b.parity][:, head, qt * P:(qt + 1) * P]
            mm(out[:], q, k_stack[b.parity][:, head // 4, 0, :], start=True, stop=False)
            mm(out[:], q, k_stack[b.parity][:, head // 4, 1, :], start=False, stop=True).then_inc(scored, 1)

        def turn_probs(b, u):
            pe.wait_ge(exped, b.nth(UNITS, u + 1))
            if b.has(UNITS, u - 1):
                pe.wait_ge(turned_out, b.nth(UNITS, u - 1))
            for k in range(4):
                last = turn(ps_turned[u % 2][:, k * P:(k + 1) * P], probs[:, u % 4, k * P:(k + 1) * P], ident[:])
            last.then_inc(turned, 1)

        def attend(b, g, k):
            pair, half = g // 2, g % 2
            if k == 0:
                pe.wait_ge(turned_out, b.nth(UNITS, 4 * g + 4))
                if half == 0 and b.has(PAIRS, pair):
                    pe.wait_ge(o_copied, b.nth(PAIRS, pair))
            for j in range(2):
                kv = (2 * pair + j) // 4
                last = mm(ps_out[HD * j:HD * j + HD, half * 256:half * 256 + 256],
                          v_sb[b.parity][:, k, kv * HD:(kv + 1) * HD], probs_t[g % 2][:, j, k, :],
                          start=(k == 0), stop=(k == 3))
            if k == 3:
                last.then_inc(attended, 1)

        def inverse_rows(a):
            pe.wait_ge(inv_done, a.nth(1, 1))
            if a.has(1, 0):
                pe.wait_ge(post_dve, a.nth(TT, 0))
            for t in range(TT):
                last = turn(ps_post[0:NQ, t * P:(t + 1) * P], inv_sum[:, t, :], ident[:])
            last.then_inc(post_pe, 1)

        def spread_inverse(a, pair, alone=False):
            if pair == 0:
                pe.wait_ge(inv_lo_done, a.nth(1, 1))
            elif not alone:
                pe.wait_ge(scaled, a.nth(PAIRS, pair))
            elif pair >= 3:
                pe.wait_ge(scaled, a.nth(PAIRS, pair - 2))
            mm(spread_bank(pair, alone)[:], sel[:, pair * P:(pair + 1) * P], inv_split[:], start=True, stop=True).then_inc(post_pe, 1)

        def project(a, pair, alone=False):
            if not alone:
                pe.wait_ge(scaled, a.nth(PAIRS, PAIRS))
            pe.wait_ge(o_low, a.nth(PAIRS, pair + 1))
            mm(ps_post[:], wo_hi[:, pair, :], o_hi[:, pair % 3, :], start=(pair == 0), stop=False)
            mm(ps_post[:], wo_lo[:, pair, :], o_hi[:, pair % 3, :], start=False, stop=False)
            mm(ps_post[:], wo_hi[:, pair, :], o_lo[:, pair % 2, :], start=False, stop=(pair == PAIRS - 1)).then_inc(projected, 1)

        def turn_y(a):
            pe.wait_ge(y_copied, a.nth(1, 1))
            for t in range(TT):
                last = turn(ps_post[:, t * P:(t + 1) * P], y_t[:, t * P:(t + 1) * P], ident[:])
            last.then_inc(post_pe, 1)

        def slot(b, left=0, first=False):
            for u in range(UNITS):
                turn_probs(b, u)
                if u + 3 < UNITS:
                    scores(b, u + 3, left)
                elif left:
                    scores(b.plus(1), u + 3 - UNITS)
                if u >= 4 or not first:
                    for k in ATTEND_AT.get(u % 4, ()):
                        attend(b if u >= 4 else b.plus(-1), (u // 4 - 1) % GROUPS, k)
                if left and u == PREP_X - 1:
                    turn_x(b.plus(1))
                if left and u in job_at:
                    do_job(b.plus(1), *job_at[u])
                if not first:
                    a = b.plus(-1)
                    if u == POST_INV - 1:
                        inverse_rows(a)
                    if POST_SCALE <= u < POST_SCALE + PAIRS:
                        spread_inverse(a, u - POST_SCALE)
                    if POST_PROJ <= u < POST_PROJ + PAIRS:
                        project(a, u - POST_PROJ)
                    if u == POST_Y + 1:
                        turn_y(a)

        c = Batch(0)
        pe.wait_ge(ident_loaded, 16)
        turn_x(c)
        pe.wait_ge(b_loaded, 4 * 16)
        for o in range(OCH):
            turn(ps_scores[o // 4][0:RANK, o % 4 * P:(o % 4 + 1) * P], b_raw[:, o, :], ident[:])
        turn(ps_turned[0][0:RANK, 0:P], b_raw[:, OCH, :], ident[:]).then_inc(set_pe, 1)
        pe.wait_ge(set_act, 1)
        pe.wait_ge(w_loaded, 7 * 16)
        for o in range(OCH):
            out = ps_scores[o // 4][:, o % 4 * P:(o % 4 + 1) * P]
            mm(out, w_raw[:, o, :], ident[:], start=True, stop=False)
            last = mm(out, lora_a[:, lora_of(o), :], lora_b[:, o, :], start=False, stop=True)
            if o % 4 == 3:
                last.then_inc(set_pe, 1)
        pe.wait_ge(set_dve, 7)
        for j, job in enumerate(jobs):
            if job == ("turn", 0):
                pe.wait_ge(wo_loaded, 16)
                for o in range(PAIRS):
                    out = (ps_out, ps_post)[o // 4][:, o % 4 * P:(o % 4 + 1) * P]
                    mm(out, wo_raw[:, o * P:(o + 1) * P], ident[:], start=True, stop=False)
                    last = mm(out, oa_raw[:, o * P:(o + 1) * P], lora_b[:, OCH, :], start=False, stop=True)
                last.then_inc(set_pe, 1)
            do_job(c, j, job)
        for u in range(3):
            scores(c, u)
        pe.wait_ge(set_dve, 9)
        slots(pe, slot)
        a = Batch(NB - 1)
        for k in range(4):
            attend(a, GROUPS - 1, k)
        inverse_rows(a)
        for pair in range(PAIRS + 3):
            if pair >= 3:
                project(a, pair - 3, alone=True)
            if pair < PAIRS:
                spread_inverse(a, pair, alone=True)
        turn_y(a)


def experts_block(nc, ctx, args, x1_dram, out):
    router_w, router_b, w1, b1, w2, b2, sw1, sb1, sw2, sb2, ident_d = args
    NB, S, D = x1_dram.shape
    TT = S // P
    EC = NE * EH // P
    EPC = P // EH
    SC = ES * HS // P
    CHUNKS = EC + SC
    LEAD = 4
    RING = LEAD + 1
    assert D == P and CHUNKS % RING == 0

    def sb(name, shape, dt=F32):
        return ctx.enter_context(nc.sbuf_tensor(name, shape, dt))

    def psum(name):
        return ctx.enter_context(nc.psum_tensor(name, [P, 512], F32))

    def sem(name):
        return ctx.enter_context(nc.semaphore(name))

    w1_sb = sb("w1_sb", [P, CHUNKS * P])
    w1_hi = sb("w1_hi", [P, CHUNKS * P], F32R)
    w1_lo = sb("w1_lo", [P, CHUNKS * P], F32R)
    w2_sb = sb("w2_sb", [P, CHUNKS, D])
    w2_hi = sb("w2_hi", [P, CHUNKS, D], F32R)
    w2_lo = sb("w2_lo", [P, CHUNKS, D], F32R)
    bias_rows = sb("bias_rows", [CHUNKS + ES, P])
    bias_cols = sb("bias_cols", [P, CHUNKS + ES])
    sb2_sum = sb("sb2_sum", [P, 1])
    b2_sb = sb("b2_sb", [P, D])
    b2_hi = sb("b2_hi", [P, D], F32R)
    b2_lo = sb("b2_lo", [P, D], F32R)
    router_sb = sb("router_sb", [P, NE])
    router_bias = sb("router_bias", [P, NE])
    spread_raw = sb("spread_raw", [P, EC * P])
    spread = sb("spread", [P, EC * P], F32R)
    ident2 = sb("ident2", [P, P])
    xe_in = sb("xe_in", [P, TT, D])
    xe_norm = sb("xe_norm", [P, TT, D])
    xe_t = sb("xe_t", [P, S])
    xe_hi = [sb(f"xe_hi{i}", [P, S], F32R) for i in range(2)]
    xe_lo = [sb(f"xe_lo{i}", [P, S], F32R) for i in range(2)]
    weight_t = [sb(f"weight_t{i}", [P, S], F32R) for i in range(2)]
    hidden = sb("hidden", [P, RING, S])
    gated = sb("gated", [P, RING, S])
    gated_hi = sb("gated_hi", [P, RING, S], F32R)
    gated_lo = sb("gated_lo", [P, RING, S], F32R)
    logits = sb("logits", [P, TT, NE])
    expo = sb("expo", [P, TT, NE])
    chosen = sb("chosen", [P, TT, NE])
    weights = sb("weights", [P, TT, NE])
    weight_split = sb("weight_split", [P, TT, 2, NE])
    top8 = sb("top8", [P, TT, TOPK])
    small = sb("small", [P, 5, TT])
    ye_t = sb("ye_t", [P, S])
    xe_again = sb("xe_again", [P, TT, D])
    out_sb = sb("out_sb", [P, TT, D])
    stats = sb("stats2", [P, 2, TT, 6])
    mean_var = sb("mean_var2", [P, 2, TT, 2])
    rstd = sb("rstd2", [P, 2, TT])
    minus_half = sb("minus_half2", [P, TT])
    eps = sb("eps2", [P, TT])

    ps_hidden = [psum(f"ps_hidden{i}") for i in range(2)]
    ps_weight = [psum(f"ps_weight{i}") for i in range(3)]
    ps_y = [psum(f"ps_y{i}") for i in range(2)]
    ps_prep = psum("ps_prep2")

    loaded_small = sem("loaded_small")
    loaded_w1 = sem("loaded_w1")
    loaded_w2 = sem("loaded_w2")
    set_pool = sem("set_pool")
    set_pe2 = sem("set_pe2")
    set_act2 = sem("set_act2")
    set_dve2 = sem("set_dve2")
    xe_loaded = sem("xe_loaded")
    norm_dve = sem("norm_dve")
    norm_stat = sem("norm_stat")
    norm_rstd = sem("norm_rstd")
    pool_chain2 = sem("pool_chain2")
    prep_pe2 = sem("prep_pe2")
    xe_copied = sem("xe_copied")
    split_dve = sem("split_dve")
    route_dve = sem("route_dve")
    route_exp = sem("route_exp")
    weight_ready = sem("weight_ready")
    up_done = sem("up_done")
    activated = sem("activated")
    weighted = sem("weighted")
    gated_hi_done = sem("gated_hi_done")
    gated_lo_done = sem("gated_lo_done")
    down_done = sem("down_done")
    ye_copied = sem("ye_copied")
    post_pe2 = sem("post_pe2")
    post_stat2 = sem("post_stat2")
    post_rstd2 = sem("post_rstd2")
    post_dve2 = sem("post_dve2")
    xe_again_loaded = sem("xe_again_loaded")
    out_done = sem("out_done")
    out_stored = sem("out_stored")

    N_STATS, N_OUT, N_TURN, N_SPLIT, R_LOGITS, R_SHIFT, R_EXP = 0, 2, 4, 5, 5, 6, 7
    R_PROBS, R_TOP, R_MATCH, R_PICK, R_WEIGH, R_LO, R_TURN, R_COPY = 8, 9, 10, 11, 12, 13, 14, 14
    Y_TURN, Y_STATS, Y_NORM, Y_SUM = 1, 3, 16, 18
    PREP_PE = 3
    ROUTE = 11

    x1_tiles = x1_dram.rearrange("b (t p) d -> p (b t) d", p=P)
    out_tiles = out.rearrange("b (t p) d -> p (b t) d", p=P)
    block = ctx.enter_context(nc.Block())

    def slots(eng, slot):
        slot(Batch(0), first=True, left=NB - 1)
        slot(Batch(1), left=NB - 2)
        if NB > 4:
            with eng.Fori(0, NB // 2 - 2) as i:
                slot(Batch(2, i), left=2)
                slot(Batch(3, i), left=2)
        slot(Batch(NB - 2), left=1)
        slot(Batch(NB - 1), left=0)

    @block.sync
    def _(sp):
        sp.dma_start(xe_in[:], x1_tiles[:, 0:TT, :]).then_inc(xe_loaded, 16)
        sp.dma_start(ident2[:], ident_d).then_inc(loaded_small, 16)
        sp.dma_start(router_sb[:], router_w).then_inc(loaded_small, 16)
        sp.dma_start(router_bias[:], router_b.partition_broadcast(P)).then_inc(loaded_small, 16)
        sp.dma_start(bias_rows[0:EC, :], b1.rearrange("(c e) h -> c (e h)", e=EPC)).then_inc(loaded_small, 16)
        sp.dma_start(bias_rows[EC:CHUNKS, :], sb1.rearrange("e (c h) -> (e c) h", h=P)).then_inc(loaded_small, 16)
        sp.dma_start(bias_rows[CHUNKS:CHUNKS + ES, :], sb2).then_inc(loaded_small, 16)
        sp.dma_start(b2_sb[0:NE, :], b2).then_inc(loaded_small, 16)
        sp.dma_start(b2_sb[NE:2 * NE, :], b2).then_inc(loaded_small, 16)
        sp.dma_start(w1_sb[:, 0:EC * P].rearrange("d (e h) -> d e h", e=NE), w1.rearrange("e d h -> d e h")).then_inc(loaded_w1, 16)
        sp.dma_start(w1_sb[:, EC * P:CHUNKS * P].rearrange("d (e h) -> d e h", e=ES), sw1.rearrange("e d h -> d e h")).then_inc(loaded_w1, 16)
        sp.dma_start(w2_sb[:, 0:EC, :], w2.rearrange("(c e) h d -> (e h) c d", e=EPC)).then_inc(loaded_w2, 16)
        sp.dma_start(w2_sb[:, EC:CHUNKS, :], sw2.rearrange("e (c h) d -> h (e c) d", h=P)).then_inc(loaded_w2, 16)

        def load_x1(c):
            sp.wait_ge(norm_dve, c.nth(1, 0))
            sp.dma_start(xe_in[:], x1_tiles[:, bass.ds(c.index() * TT, TT), :]).then_inc(xe_loaded, 16)

        def load_again(a):
            if a.has(1, 0):
                sp.wait_ge(out_done, a.nth(1, 0))
            sp.dma_start(xe_again[:], x1_tiles[:, bass.ds(a.index() * TT, TT), :]).then_inc(xe_again_loaded, 16)

        def store(a):
            sp.wait_ge(out_done, a.nth(1, 1))
            sp.dma_start(out_tiles[:, bass.ds(a.index() * TT, TT), :], out_sb[:]).then_inc(out_stored, 16)

        def slot(b, left=0, first=False):
            if left >= 2:
                load_x1(b.plus(2))
            if not first:
                load_again(b.plus(-1))
                store(b.plus(-1))

        load_x1(Batch(1))
        slots(sp, slot)
        load_again(Batch(NB - 1))
        store(Batch(NB - 1))
        sp.wait_ge(out_stored, 16 * NB)

    @block.gpsimd
    def _(pool):
        nc.gpsimd.memset(minus_half[:], -0.5)
        nc.gpsimd.memset(eps[:], EPS)
        nc.gpsimd.memset(spread_raw[:], 0.0).then_inc(set_pool, 1)
        pool.wait_ge(set_pool, 1)
        view = spread_raw[:].rearrange("p (c e h) -> p c e h", c=EC, e=EPC)
        for half in range(2):
            nc.gpsimd.affine_select(out=view, in_=view, compare_op=ALU.not_equal, fill=1.0, base=-half * NE,
                                    pattern=[[-EPC, EC], [-1, EPC], [0, EH]], channel_multiplier=1).then_inc(set_pool, 1)
            pool.wait_ge(set_pool, 2 + half)

        def rstd_of(which, b, stat, done, chain_value):
            pool.wait_ge(stat, b.nth(1, 1))
            nc.gpsimd.tensor_tensor(rstd[:, which, :], mean_var[:, which, :, 1], eps[:], ALU.add).then_inc(pool_chain2, 1)
            pool.wait_ge(pool_chain2, chain_value)
            nc.gpsimd.tensor_tensor(rstd[:, which, :], rstd[:, which, :], minus_half[:], ALU.pow).then_inc(done, 1)

        def gate_lo(b, c):
            pool.wait_ge(gated_hi_done, b.nth(CHUNKS, c + 1))
            if b.has(CHUNKS, c + 1 - RING):
                pool.wait_ge(down_done, b.nth(CHUNKS, c + 1 - RING))
            nc.gpsimd.tensor_tensor(gated_lo[:, c % RING, :], gated[:, c % RING, :], gated_hi[:, c % RING, :].bitcast(F32),
                                    ALU.subtract).then_inc(gated_lo_done, 1)

        def slot(b, left=0, first=False):
            for c in range(CHUNKS):
                if c + LEAD < CHUNKS:
                    gate_lo(b, c + LEAD)
                elif left:
                    gate_lo(b.plus(1), c + LEAD - CHUNKS)
                if left and c == N_STATS:
                    rstd_of(0, b.plus(1), norm_stat, norm_rstd, 2 if first else b.nth(2, 1))
                if not first and c == Y_STATS:
                    rstd_of(1, b.plus(-1), post_stat2, post_rstd2, b.nth(2, 2 if left else 1))

        rstd_of(0, Batch(0), norm_stat, norm_rstd, 1)
        for c in range(LEAD):
            gate_lo(Batch(0), c)
        slots(pool, slot)
        rstd_of(1, Batch(NB - 1), post_stat2, post_rstd2, 2 * NB)

    @block.scalar
    def _(act):
        act.wait_ge(set_pe2, 1)
        nc.scalar.activation(bias_cols[:], ps_y[0][:, 0:CHUNKS + ES], ACT.Copy).then_inc(set_act2, 1)
        act.wait_ge(set_act2, 1)
        act.wait_ge(set_dve2, 1)

        def copy_x(c):
            act.wait_ge(prep_pe2, c.nth(PREP_PE, 1))
            if c.has(2, 0):
                act.wait_ge(split_dve, c.nth(2, 0))
            nc.scalar.activation(xe_t[:], ps_prep[:], ACT.Copy).then_inc(xe_copied, 1)

        def activate(b, c):
            act.wait_ge(up_done, b.nth(CHUNKS, c + 1))
            if c < EC:
                if b.has(EC, max(c + 1 - RING, 0)):
                    act.wait_ge(weighted, b.nth(EC, max(c + 1 - RING, 0)))
                dst = hidden
            else:
                act.wait_ge(gated_lo_done, b.nth(CHUNKS, c + 1 - RING))
                dst = gated
            nc.scalar.activation(dst[:, c % RING, :], ps_hidden[c % 2][:], ACT.Silu, bias=bias_cols[:, c:c + 1]).then_inc(activated, 1)

        def gate_hi(b, c):
            if c < EC:
                act.wait_ge(weighted, b.nth(EC, c + 1))
            else:
                act.wait_ge(activated, b.nth(CHUNKS, c + 1))
            if b.has(CHUNKS, c + 1 - RING):
                act.wait_ge(down_done, b.nth(CHUNKS, c + 1 - RING))
            nc.scalar.activation(gated_hi[:, c % RING, :], gated[:, c % RING, :], ACT.Copy).then_inc(gated_hi_done, 1)

        def exponentials(c):
            act.wait_ge(route_dve, c.nth(ROUTE, 3))
            nc.scalar.activation(expo[:], logits[:], ACT.Exp).then_inc(route_exp, 1)

        def copy_y(b):
            act.wait_ge(down_done, b.nth(CHUNKS, CHUNKS))
            if b.has(1, 0):
                act.wait_ge(post_pe2, b.nth(1, 0))
            nc.scalar.activation(ye_t[:], ps_y[b.parity][:], ACT.Identity, bias=sb2_sum[:, 0:1]).then_inc(ye_copied, 1)

        def slot(b, left=0, first=False):
            for c in range(CHUNKS):
                if not first and c == 0:
                    copy_y(b.plus(-1))
                if c + LEAD < CHUNKS:
                    activate(b, c + LEAD)
                elif left:
                    activate(b.plus(1), c + LEAD - CHUNKS)
                if c + LEAD - 1 < CHUNKS:
                    gate_hi(b, c + LEAD - 1)
                elif left:
                    gate_hi(b.plus(1), c + LEAD - 1 - CHUNKS)
                if left and c == N_TURN:
                    copy_x(b.plus(1))
                if left and c == R_EXP:
                    exponentials(b.plus(1))

        copy_x(Batch(0))
        exponentials(Batch(0))
        for c in range(LEAD):
            activate(Batch(0), c)
        for c in range(LEAD - 1):
            gate_hi(Batch(0), c)
        slots(act, slot)
        copy_y(Batch(NB - 1))

    @block.vector
    def _(dve):
        def variance(which, src, stat):
            for t in range(TT):
                nc.vector.bn_stats(stats[:, which, t, :], src[:, t, :])
            dve.drain()
            for t in range(TT):
                last = nc.vector.bn_aggr(mean_var[:, which, t, :], stats[:, which, t, :])
            last.then_inc(stat, 1)

        def normalise(which, out, src, t):
            return nc.vector.tensor_scalar(out[:, t, :], src[:, t, :], mean_var[:, which, t, 0:1], rstd[:, which, t:t + 1],
                                           ALU.subtract, ALU.mult)

        def norm_x(c):
            dve.wait_ge(xe_loaded, c.nth(16, 16))
            variance(0, xe_in, norm_stat)

        def norm_out(c):
            dve.wait_ge(norm_rstd, c.nth(1, 1))
            if c.has(PREP_PE, 1 - PREP_PE):
                dve.wait_ge(prep_pe2, c.nth(PREP_PE, 1 - PREP_PE))
            for t in range(TT):
                last = normalise(0, xe_norm, xe_in, t)
            last.then_inc(norm_dve, 1)

        def split_x(c):
            dve.wait_ge(xe_copied, c.nth(1, 1))
            if c.has(CHUNKS, -CHUNKS):
                dve.wait_ge(up_done, c.nth(CHUNKS, -CHUNKS))
            nc.vector.tensor_copy(xe_hi[c.parity][:], xe_t[:]).then_inc(split_dve, 1)
            dve.wait_ge(split_dve, c.nth(2, 1))
            nc.vector.tensor_tensor(xe_lo[c.parity][:], xe_t[:], xe_hi[c.parity][:].bitcast(F32), ALU.subtract).then_inc(split_dve, 1)

        def per_token(k):
            return small[:, k, :].unsqueeze(2).to_broadcast([P, TT, NE])

        def shift_logits(c):
            dve.wait_ge(prep_pe2, c.nth(PREP_PE, 2))
            bias = router_bias[:].unsqueeze(1).to_broadcast([P, TT, NE])
            nc.vector.tensor_tensor(logits[:], ps_prep[:, 0:TT * NE].rearrange("p (t e) -> p t e", t=TT), bias, ALU.add).then_inc(route_dve, 1)
            dve.wait_ge(route_dve, c.nth(ROUTE, 1))
            nc.vector.reduce_max(small[:, 0, :], logits[:], AX_X, negate=True).then_inc(route_dve, 1)
            dve.wait_ge(route_dve, c.nth(ROUTE, 2))
            nc.vector.tensor_tensor(logits[:], logits[:], per_token(0), ALU.add).then_inc(route_dve, 1)

        def probabilities(c):
            dve.wait_ge(route_exp, c.nth(1, 1))
            nc.vector.reduce_sum(small[:, 1, :], expo[:], AX_X).then_inc(route_dve, 1)
            dve.wait_ge(route_dve, c.nth(ROUTE, 4))
            nc.vector.reciprocal(small[:, 2, :], small[:, 1, :]).then_inc(route_dve, 1)
            dve.wait_ge(route_dve, c.nth(ROUTE, 5))
            nc.vector.tensor_tensor(expo[:], expo[:], per_token(2), ALU.mult).then_inc(route_dve, 1)

        def top(c):
            dve.drain()
            for t in range(TT):
                last = nc.vector.max(top8[:, t, :], expo[:, t, :])
            last.then_inc(route_dve, 1)

        def match(c):
            dve.wait_ge(route_dve, c.nth(ROUTE, 7))
            nc.vector.reduce_sum(small[:, 3, :], top8[:], AX_X)
            for t in range(TT):
                last = nc.vector.match_replace(chosen[:, t, :], top8[:, t, :], expo[:, t, :], -1.0)
            last.then_inc(route_dve, 1)

        def pick(c):
            dve.wait_ge(route_dve, c.nth(ROUTE, 8))
            nc.vector.scalar_tensor_tensor(weights[:], chosen[:], 0.0, expo[:], ALU.is_lt, ALU.mult)
            nc.vector.reciprocal(small[:, 4, :], small[:, 3, :]).then_inc(route_dve, 1)

        def weigh(c):
            dve.wait_ge(route_dve, c.nth(ROUTE, 9))
            nc.vector.tensor_tensor(weights[:], weights[:], per_token(4), ALU.mult).then_inc(route_dve, 1)
            dve.wait_ge(route_dve, c.nth(ROUTE, 10))
            if c.has(PREP_PE, 0):
                dve.wait_ge(prep_pe2, c.nth(PREP_PE, 0))
            nc.vector.tensor_copy(weight_split[:, :, 0, :].bitcast(F32R), weights[:]).then_inc(weight_ready, 1)

        def weigh_lo(c):
            dve.wait_ge(weight_ready, c.nth(2, 1))
            nc.vector.tensor_tensor(weight_split[:, :, 1, :], weights[:], weight_split[:, :, 0, :], ALU.subtract).then_inc(weight_ready, 1)

        def copy_weights(c):
            dve.wait_ge(prep_pe2, c.nth(PREP_PE, 3))
            if c.has(CHUNKS, -CHUNKS):
                dve.wait_ge(down_done, c.nth(CHUNKS, -CHUNKS))
            nc.vector.tensor_copy(weight_t[c.parity][:], ps_prep[:]).then_inc(route_dve, 1)

        def weigh_hidden(b, c):
            dve.wait_ge(activated, b.nth(CHUNKS, c + 1))
            if b.has(CHUNKS, c + 1 - RING):
                dve.wait_ge(gated_lo_done, b.nth(CHUNKS, c + 1 - RING))
            nc.vector.tensor_tensor(gated[:, c % RING, :], hidden[:, c % RING, :], ps_weight[c % 3][:], ALU.mult).then_inc(weighted, 1)


        def y_stats(a):
            dve.wait_ge(post_pe2, a.nth(1, 1))
            variance(1, ps_y[a.parity][:].rearrange("p (t d) -> p t d", t=TT), post_stat2)

        def y_norm(a):
            dve.wait_ge(post_rstd2, a.nth(1, 1))
            if a.has(16, 0):
                dve.wait_ge(out_stored, a.nth(16, 0))
            for t in range(TT):
                last = normalise(1, out_sb, ps_y[a.parity][:].rearrange("p (t d) -> p t d", t=TT), t)
            last.then_inc(post_dve2, 1)

        def y_sum(a):
            dve.wait_ge(post_dve2, a.nth(1, 1))
            dve.wait_ge(xe_again_loaded, a.nth(16, 16))
            nc.vector.tensor_tensor(out_sb[:], out_sb[:], xe_again[:], ALU.add).then_inc(out_done, 1)

        ROUTER = [(N_STATS, norm_x), (N_OUT, norm_out), (N_SPLIT, split_x), (R_SHIFT, shift_logits), (R_PROBS, probabilities),
                  (R_TOP, top), (R_MATCH, match), (R_PICK, pick), (R_WEIGH, weigh), (R_LO, weigh_lo), (R_COPY, copy_weights)]

        def slot(b, left=0, first=False):
            for c in range(CHUNKS):
                if c + LEAD < EC:
                    weigh_hidden(b, c + LEAD)
                elif left and c + LEAD >= CHUNKS:
                    weigh_hidden(b.plus(1), c + LEAD - CHUNKS)
                for step, stage in ROUTER:
                    if left and c == step:
                        stage(b.plus(1))
                if not first and c == Y_STATS:
                    y_stats(b.plus(-1))
                if not first and c == Y_NORM:
                    y_norm(b.plus(-1))
                if not first and c == Y_SUM:
                    y_sum(b.plus(-1))

        c = Batch(0)
        dve.wait_ge(loaded_small, 8 * 16)
        norm_x(c)
        norm_out(c)
        dve.wait_ge(set_act2, 1)
        nc.vector.tensor_tensor(sb2_sum[:], bias_cols[:, CHUNKS:CHUNKS + 1], bias_cols[:, CHUNKS + 1:CHUNKS + 2], ALU.add).then_inc(set_dve2, 1)
        nc.vector.tensor_copy(b2_hi[:], b2_sb[:]).then_inc(set_dve2, 1)
        dve.wait_ge(set_dve2, 2)
        nc.vector.tensor_tensor(b2_lo[:], b2_sb[:], b2_hi[:].bitcast(F32), ALU.subtract).then_inc(set_dve2, 1)
        split_x(c)
        shift_logits(c)
        probabilities(c)
        top(c)
        match(c)
        pick(c)
        weigh(c)
        weigh_lo(c)
        dve.wait_ge(loaded_w1, 32)
        nc.vector.tensor_copy(w1_hi[:], w1_sb[:]).then_inc(set_dve2, 1)
        dve.wait_ge(set_dve2, 4)
        nc.vector.tensor_tensor(w1_lo[:], w1_sb[:], w1_hi[:].bitcast(F32), ALU.subtract).then_inc(set_dve2, 1)
        dve.wait_ge(set_pool, 3)
        nc.vector.tensor_copy(spread[:], spread_raw[:]).then_inc(set_dve2, 1)
        dve.wait_ge(loaded_w2, 32)
        nc.vector.tensor_copy(w2_hi[:], w2_sb[:]).then_inc(set_dve2, 1)
        dve.wait_ge(set_dve2, 7)
        nc.vector.tensor_tensor(w2_lo[:], w2_sb[:], w2_hi[:].bitcast(F32), ALU.subtract).then_inc(set_dve2, 1)
        copy_weights(c)
        for k in range(LEAD):
            weigh_hidden(c, k)
        slots(dve, slot)
        y_stats(Batch(NB - 1))
        y_norm(Batch(NB - 1))
        y_sum(Batch(NB - 1))

    @block.tensor
    def _(pe):
        mm, turn = nc.tensor.matmul, nc.tensor.transpose

        def turn_x(c):
            pe.wait_ge(norm_dve, c.nth(1, 1))
            if c.has(ROUTE, 0):
                pe.wait_ge(route_dve, c.nth(ROUTE, 0))
            for t in range(TT):
                last = turn(ps_prep[:, t * P:(t + 1) * P], xe_norm[:, t, :], ident2[:])
            last.then_inc(prep_pe2, 1)

        def make_logits(c):
            pe.wait_ge(xe_copied, c.nth(1, 1))
            for t in range(TT):
                last = mm(ps_prep[:, t * NE:(t + 1) * NE], xe_t[:, t * P:(t + 1) * P], router_sb[:], start=True, stop=True)
            last.then_inc(prep_pe2, 1)

        def turn_weights(c):
            pe.wait_ge(weight_ready, c.nth(2, 2))
            for t in range(TT):
                last = turn(ps_prep[:, t * P:(t + 1) * P], weight_split[:, t, :, :].rearrange("p a e -> p (a e)"), ident2[:])
            last.then_inc(prep_pe2, 1)

        def up(b, c):
            if c == 0:
                pe.wait_ge(split_dve, b.nth(2, 2))
                pe.wait_ge(route_dve, b.nth(ROUTE, ROUTE))
            if b.has(CHUNKS, c - 1):
                pe.wait_ge(activated, b.nth(CHUNKS, c - 1))
            if c < EC:
                if b.has(EC, max(c - 2, 0)):
                    pe.wait_ge(weighted, b.nth(EC, max(c - 2, 0)))
                mm(ps_weight[c % 3][:], spread[:, c * P:(c + 1) * P], weight_t[b.parity][:], start=True, stop=True)
            cols = slice(c * P, (c + 1) * P)
            out = ps_hidden[c % 2][:]
            mm(out, w1_hi[:, cols], xe_hi[b.parity][:], start=True, stop=False)
            mm(out, w1_hi[:, cols], xe_lo[b.parity][:], start=False, stop=False)
            mm(out, w1_lo[:, cols], xe_hi[b.parity][:], start=False, stop=True).then_inc(up_done, 1)

        def down(b, c):
            out = ps_y[b.parity][:]
            if c == 0:
                if b.has(1, -1):
                    pe.wait_ge(post_dve2, b.nth(1, -1))
                mm(out, b2_hi[:], weight_t[b.parity][:], start=True, stop=False)
                mm(out, b2_lo[:], weight_t[b.parity][:], start=False, stop=False)
            pe.wait_ge(gated_hi_done, b.nth(CHUNKS, c + 1))
            mm(out, w2_hi[:, c, :], gated_hi[:, c % RING, :], start=False, stop=False)
            mm(out, w2_lo[:, c, :], gated_hi[:, c % RING, :], start=False, stop=False)
            pe.wait_ge(gated_lo_done, b.nth(CHUNKS, c + 1))
            mm(out, w2_hi[:, c, :], gated_lo[:, c % RING, :], start=False, stop=(c == CHUNKS - 1)).then_inc(down_done, 1)

        def turn_y(a):
            pe.wait_ge(ye_copied, a.nth(1, 1))
            for t in range(TT):
                last = turn(ps_y[a.parity][:, t * P:(t + 1) * P], ye_t[:, t * P:(t + 1) * P], ident2[:])
            last.then_inc(post_pe2, 1)

        def slot(b, left=0, first=False):
            for c in range(CHUNKS):
                down(b, c)
                if c + LEAD < CHUNKS:
                    up(b, c + LEAD)
                elif left:
                    up(b.plus(1), c + LEAD - CHUNKS)
                if left and c == N_TURN:
                    turn_x(b.plus(1))
                if left and c == R_LOGITS:
                    make_logits(b.plus(1))
                if left and c == R_TURN:
                    turn_weights(b.plus(1))
                if not first and c == Y_TURN:
                    turn_y(b.plus(-1))

        pe.wait_ge(loaded_small, 8 * 16)
        turn(ps_y[0][:, 0:CHUNKS + ES], bias_rows[:], ident2[0:CHUNKS + ES, 0:CHUNKS + ES]).then_inc(set_pe2, 1)
        c = Batch(0)
        turn_x(c)
        make_logits(c)
        turn_weights(c)
        pe.wait_ge(set_dve2, 6)
        for k in range(LEAD):
            up(c, k)
        pe.wait_ge(set_act2, 1)
        pe.wait_ge(set_dve2, 8)
        slots(pe, slot)
        turn_y(Batch(NB - 1))


def layer_kernel(nc, x, Wq, Wk, Wv, Wo, qA, qB, kA, kB, vA, vB, oA, oB, router_w, router_b,
                 w1, b1, w2, b2, sw1, sb1, sw2, sb2, cos_t, sin_t, ident_d, sel_d, out):
    x1_dram = nc.dram_tensor("x_after_attention", x.shape, F32, kind="Internal").ap()
    with ExitStack() as ctx:
        attention_block(nc, ctx, (x, Wq, Wk, Wv, Wo, qA, qB, kA, kB, vA, vB, oA, oB, cos_t, sin_t, ident_d, sel_d), x1_dram)
    with ExitStack() as ctx:
        experts_block(nc, ctx, (router_w, router_b, w1, b1, w2, b2, sw1, sb1, sw2, sb2, ident_d), x1_dram, out)


_INS = ['L0_attn_x', 'L0_attn_Wq', 'L0_attn_Wk', 'L0_attn_Wv', 'L0_attn_Wo', 'L0_attn_qA', 'L0_attn_qB', 'L0_attn_kA',
        'L0_attn_kB', 'L0_attn_vA', 'L0_attn_vB', 'L0_attn_oA', 'L0_attn_oB', 'L0_ffn_router_w', 'L0_ffn_router_b',
        'L0_ffn_w1', 'L0_ffn_b1', 'L0_ffn_w2', 'L0_ffn_b2', 'L0_ffn_sw1', 'L0_ffn_sb1', 'L0_ffn_sw2', 'L0_ffn_sb2']


def _constants(seq):
    import numpy as np
    inv_freq = (1.0 / np.float32(10000.0) ** (np.arange(0, HD, 2, dtype=np.float32) / np.float32(HD))).astype(np.float32)
    freqs = np.arange(seq, dtype=np.float32)[:, None] * inv_freq[None, :]
    def tiled(a):
        return np.ascontiguousarray(a.astype(np.float32).reshape(seq // P, P, HALF).transpose(1, 0, 2))
    pair_head = np.arange(NQ * HD) // HD
    sel = np.zeros((32 + NQ, NQ * HD), np.float32)
    sel[0:NQ] = sel[32:32 + NQ] = np.arange(NQ)[:, None] == pair_head[None, :]
    return {'cos': tiled(np.cos(freqs)), 'sin': tiled(np.sin(freqs)), 'ident': np.eye(P, dtype=np.float32), 'sel': sel}


def kernel(**inputs):
    import numpy as _np
    import concourse.bacc as _bacc
    from concourse import mybir as _mybir
    from concourse.bass_utils import run_bass_kernel_spmd as _run

    nc = _bacc.Bacc("TRN2", target_bir_lowering=False, num_devices=1)
    arrays = {f"in_{name}_dram": _np.ascontiguousarray(inputs[name]) for name in _INS}
    shape = inputs['L0_attn_x'].shape
    arrays.update({f"const_{name}_dram": a for name, a in _constants(shape[1]).items()})
    args = [nc.dram_tensor(name, a.shape, _mybir.dt.from_np(a.dtype), kind="ExternalInput").ap()
            for name, a in arrays.items()]
    args.append(nc.dram_tensor("out_0_dram", shape, _mybir.dt.float32, kind="ExternalOutput").ap())
    layer_kernel(nc, *args)
    r = _run(nc, [arrays], core_ids=[0])
    return r.results[0]["out_0_dram"]
```
